# Optimizing a Trainium2 kernel written in Bass

```python
import numpy as np
import jax
import jax.numpy as jnp

def _softmax(x, axis=-1):
    return jax.nn.softmax(x, axis=axis)

def _gelu(x):
    return jax.nn.gelu(x, approximate=True)

def _silu(x):
    return jax.nn.silu(x)

def _sigmoid(x):
    return jax.nn.sigmoid(x)

def _layernorm(x, axis=-1, eps=1e-05):
    m = jnp.mean(x, axis=axis, keepdims=True)
    v = jnp.var(x, axis=axis, keepdims=True)
    return (x - m) / jnp.sqrt(v + eps)

def _scatter_add(tgt, idx, src, axis=0):
    return tgt.at[idx].add(src)

def _segment_sum(src, seg, n):
    return jax.ops.segment_sum(src, seg, n)
kernel_name = 'mk_adj_ffn_d1_adj_r2_775339'

def setup_inputs(seed: int=0):
    np.random.seed(seed)
    _w = jnp.asarray

    def _rec_inputs():
        import jax
        import jax.numpy as jnp
        _gk = jax.random.key(seed)
        x = 7.22e-05 + 1 * jax.random.normal(jax.random.fold_in(_gk, 1), (1354, 512), jnp.float32)
        _a = jax.random.bernoulli(jax.random.fold_in(_gk, 2), 0.00295421, (1354, 1354))
        _a = jnp.logical_or(_a, jnp.swapaxes(_a, -1, -2))
        _a = jnp.logical_or(_a, jnp.eye(1354, dtype=bool))
        _af = _a.astype(jnp.float32)
        _d = jnp.maximum(_af.sum(-1), 1.0) ** (-0.5)
        _af = _af * _d[..., :, None] * _d[..., None, :]
        adj = _af
        return (x, adj)
    x, adj = _rec_inputs()

    def _L0_gnn_setup():
        import jax, jax.numpy as jnp
        import numpy as np
        N = 4096
        D = 512

        def adjacent_mat(adj):
            adj = adj + jnp.eye(adj.shape[0], dtype=adj.dtype)
            deg = jnp.sum(adj, axis=1)
            dinv = jnp.where(deg > 0, deg ** (-0.5), 0.0).astype(adj.dtype)
            return dinv[:, None] * adj * dinv[None, :]
        key = jax.random.key(seed)
        k1, k2 = jax.random.split(key)
        x = jax.random.normal(k1, (N, D), dtype=jnp.float32)
        Coefficient2 = 1e-08 * jnp.ones((N, N), dtype=jnp.float32)
        A = jax.random.uniform(k2, (N, N), dtype=jnp.float32)
        return {'x': x, 'Coefficient2': Coefficient2, 'A': A}
    _L0_gnn_all = _L0_gnn_setup()
    _L0_gnn_in = {k: v for k, v in _L0_gnn_all.items() if k in ()}
    del _L0_gnn_all

    def _L0_ffn_setup():
        import jax, jax.numpy as jnp
        import numpy as np
        D_MODEL = 512
        D_FF = 2048
        N_EXPERTS = 8
        TOP_K = 2
        D_FF_PER = D_FF // N_EXPERTS
        B, T = (4, 1024)
        key = jax.random.key(seed)
        ks = jax.random.split(key, 7)
        b1_bound = 1.0 / np.sqrt(D_MODEL)
        b2_bound = 1.0 / np.sqrt(D_FF_PER)
        return {'x': jax.random.normal(ks[0], (B, T, D_MODEL), dtype=jnp.float32), 'router_w': jax.random.uniform(ks[1], (D_MODEL, N_EXPERTS), minval=-b1_bound, maxval=b1_bound, dtype=jnp.float32), 'router_b': jax.random.uniform(ks[2], (N_EXPERTS,), minval=-b1_bound, maxval=b1_bound, dtype=jnp.float32), 'W1': jax.random.uniform(ks[3], (N_EXPERTS, D_MODEL, D_FF_PER), minval=-b1_bound, maxval=b1_bound, dtype=jnp.float32), 'b1': jax.random.uniform(ks[4], (N_EXPERTS, D_FF_PER), minval=-b1_bound, maxval=b1_bound, dtype=jnp.float32), 'W2': jax.random.uniform(ks[5], (N_EXPERTS, D_FF_PER, D_MODEL), minval=-b2_bound, maxval=b2_bound, dtype=jnp.float32), 'b2': jax.random.uniform(ks[6], (N_EXPERTS, D_MODEL), minval=-b2_bound, maxval=b2_bound, dtype=jnp.float32)}
    _L0_ffn_all = _L0_ffn_setup()
    _L0_ffn_in = {k: v for k, v in _L0_ffn_all.items() if k in ('router_w', 'router_b', 'W1', 'b1', 'W2', 'b2')}
    del _L0_ffn_all
    return {'x': x, 'adj': adj, 'L0_ffn_router_w': _L0_ffn_in['router_w'], 'L0_ffn_router_b': _L0_ffn_in['router_b'], 'L0_ffn_W1': _L0_ffn_in['W1'], 'L0_ffn_b1': _L0_ffn_in['b1'], 'L0_ffn_W2': _L0_ffn_in['W2'], 'L0_ffn_b2': _L0_ffn_in['b2']}

def reference(x, adj, L0_ffn_router_w, L0_ffn_router_b, L0_ffn_W1, L0_ffn_b1, L0_ffn_W2, L0_ffn_b2):
    import jax
    import jax.numpy as jnp

    def _L0_gnn_ref(x, Coefficient2, A):
        import jax, jax.numpy as jnp
        import numpy as np
        N = 4096
        D = 512

        def adjacent_mat(adj):
            adj = adj + jnp.eye(adj.shape[0], dtype=adj.dtype)
            deg = jnp.sum(adj, axis=1)
            dinv = jnp.where(deg > 0, deg ** (-0.5), 0.0).astype(adj.dtype)
            return dinv[:, None] * adj * dinv[None, :]
        A_c = jax.lax.stop_gradient(A)
        adj = adjacent_mat((A_c + A_c.T) * 0.5)
        y = Coefficient2 @ adj
        y = y @ x
        return y

    def _L0_ffn_ref(x, router_w, router_b, W1, b1, W2, b2):
        import jax, jax.numpy as jnp
        import numpy as np
        D_MODEL = 512
        D_FF = 2048
        N_EXPERTS = 8
        TOP_K = 2
        D_FF_PER = D_FF // N_EXPERTS
        B, T = (4, 1024)
        router_logits = x @ router_w + router_b
        routing_weights = jax.nn.softmax(router_logits, axis=-1)
        top_k_weights, top_k_indices = jax.lax.top_k(routing_weights, TOP_K)
        top_k_weights = top_k_weights / jnp.sum(top_k_weights, axis=-1, keepdims=True)
        routing_mask = jnp.zeros_like(routing_weights)
        routing_mask = jnp.take_along_axis(routing_mask, top_k_indices, axis=-1)
        b_idx = jnp.arange(x.shape[0])[:, None, None]
        t_idx = jnp.arange(x.shape[1])[None, :, None]
        routing_mask = jnp.zeros_like(routing_weights).at[b_idx, t_idx, top_k_indices].set(top_k_weights)
        h1 = jnp.einsum('btd,nde->btne', x, W1) + b1
        h1 = jax.nn.gelu(h1, approximate=False)
        out_per_expert = jnp.einsum('btne,nef->btnf', h1, W2) + b2
        output = jnp.sum(out_per_expert * routing_mask[..., None], axis=-2)
        return output
    x = x + _L0_gnn_ref(_layernorm(x, axis=-1), adj, adj)
    x = x + _L0_ffn_ref(_layernorm(x, axis=-1)[None], L0_ffn_router_w, L0_ffn_router_b, L0_ffn_W1, L0_ffn_b1, L0_ffn_W2, L0_ffn_b2)[0]
    return x

_drawn_inputs = setup_inputs


def setup_inputs(seed=0):
    import zlib

    import numpy as np

    out = dict(_drawn_inputs(seed))
    spreads = {}
    factors = {'L0_ffn_router_b': 2.702, 'L0_ffn_b1': 8.0}
    for name, (base, spread) in spreads.items():
        noise = np.random.default_rng([zlib.crc32(name.encode()), seed]).standard_normal(out[name].shape)
        drawn = base * np.exp(spread * noise) if base else spread * noise
        out[name] = jnp.asarray(drawn.astype(out[name].dtype))
    for name, factor in factors.items():
        out[name] = (out[name] * factor).astype(out[name].dtype)
    return out
```

```python
from contextlib import ExitStack

import concourse.bass as bass
from concourse import mybir

F32 = mybir.dt.float32
F32R = mybir.dt.float32r
F16 = mybir.dt.float16
BF16 = mybir.dt.bfloat16
I32 = mybir.dt.int32
U32 = mybir.dt.uint32
ALU = mybir.AluOpType
ACT = mybir.ActivationFunctionType
AX_X = mybir.AxisListType.X
ds = bass.ds

P = 128
N = 1354
D = 512
E = 8
FE = 256
TOP = 2
EPS = 1e-5
TILES = -(-N // P)
NP = TILES * P
DC = D // P
FC = FE // P
LAST = N - (TILES - 1) * P
SLOT_TILES = (TOP * N + E * (P - 1)) // P
ROW = D + E
STREAM = 7
KEEP = TILES - STREAM
SC = STREAM * P
KC = KEEP * P
CHUNK = 512
W2_CHUNK = E * DC * FE // CHUNK
CHUNKS = W2_CHUNK + E * FC * D // CHUNK
EARLY = 22
OUT_ROWS = N + P


def build(nc, x_rows, adj_rows, adjt_rows, adjt_cols, weights, router_w, router_b, b1, b2, out):
    with ExitStack() as ctx:
        base = -(-nc.sbuf_base // 32) * 32

        def at(name, offset, shape, dt):
            return nc.alloc_sbuf_tensor_at(name, shape, dt, offset=base + offset)

        def sem(name):
            return ctx.enter_context(nc.semaphore(name))

        def sems(name, n=2):
            return [sem(f"{name}{i}") for i in range(n)]

        ARENA = 212800
        ctx.enter_context(nc.sbuf_tensor("arena", [P, ARENA // 4], F32))
        w_hi = at("w_hi", 0, [P, CHUNKS, CHUNK], F32R)
        w_lo = at("w_lo", 65536, [P, CHUNKS, CHUNK], F32R)
        xn_t = at("xn_t", 4 * CHUNK * EARLY, [P, DC, P], F32)
        b1_all = at("b1_all", 131072, [P, E * FE], F32)
        b2_all = at("b2_all", 139264, [P, E * D], F32)
        y_hi = at("y_hi", 0, [P, TILES, D], F32R)
        y_lo = at("y_lo", 22528, [P, TILES, D], F32R)
        keep_hi = at("keep_hi", 45056, [P, TILES, KC], F32R)
        keep_lo = at("keep_lo", 67584, [P, TILES, KC], F32R)
        stream_hi = [at(f"stream_hi{u}", 90112 + 3584 * u, [P, SC], F32R) for u in range(2)]
        stream_lo = [at(f"stream_lo{u}", 97280 + 3584 * u, [P, SC], F32R) for u in range(2)]
        ZB = 110592
        z_hi = at("z_hi", ZB, [P, TILES, D], F32R)
        z_lo = at("z_lo", ZB + 22528, [P, TILES, D], F32R)
        x_row = [at(f"x_row{u}", ZB + 2048 * u, [P, D], F32) for u in range(2)]
        y_row = [at(f"y_row{u}", ZB + 4096 + 2048 * u, [P, D], F32) for u in range(2)]
        AB = 155648
        RB = 4 * NP
        a_row = [at(f"a_row{u}", AB + RB * u, [P, NP], F32) for u in range(2)]
        at_row = [at(f"at_row{u}", AB + RB * (2 + u), [P, NP], F32) for u in range(2)]
        sum_row = [at(f"sum_row{u}", AB + RB * (4 + u), [P, NP], F32) for u in range(2)]
        col = [at(f"col{u}", AB + RB * u, [P, NP], F32) for u in range(2)]
        col_hi = [at(f"col_hi{u}", AB + RB * (2 + u), [P, NP], F32R) for u in range(2)]
        col_lo = [at(f"col_lo{u}", AB + RB * (4 + u), [P, NP], F32R) for u in range(2)]
        o = AB

        def slot_buffer(name, cols, dt):
            nonlocal o
            both = [at(f"{name}{u}", o + 4 * cols * u, [P, cols], dt) for u in range(2)]
            o += 8 * cols
            return both

        xg = slot_buffer("xg", ROW, F32)
        xt_hi = slot_buffer("xt_hi", D, F32R)
        xt_lo = slot_buffer("xt_lo", D, F32R)
        h_sum = slot_buffer("h_sum", FE, F32)
        h_act = slot_buffer("h_act", FE, F32)
        ht_hi = slot_buffer("ht_hi", FE, F32R)
        ht_lo = slot_buffer("ht_lo", FE, F32R)
        y_sum = slot_buffer("y_sum", D, F32)
        y_out = slot_buffer("y_out", D, F32)
        slot_place = at("slot_place", o, [P, TILES * TOP, SLOT_TILES], F16)
        slot_token = at("slot_token", o + 1280, [P, TILES * TOP, SLOT_TILES], F16)
        start_sel = at("start_sel", o + 2560, [P, TILES * TOP, E], F32)
        over_j = at("over_j", o + 3264, [1, SLOT_TILES, E], F32)
        size_before = at("size_before", o + 4192, [P, E, E], F32)
        token_0 = at("token_0", o + 4448, [P, SLOT_TILES], F32)
        empty = at("empty", o + 4576, [P, SLOT_TILES], F32)
        assert o + 4704 <= AB + 6 * RB
        o = AB + 6 * RB

        def small(name, shape, dt=F32):
            nonlocal o
            size = {F32: 4, F32R: 4, I32: 4, U32: 4, F16: 2, BF16: 2}[dt]
            for n in shape[1:]:
                size *= n
            t = at(name, o, shape, dt)
            o += -(-size // 32) * 32
            assert o <= ARENA
            return t

        chunk = [small(f"chunk{u}", [P, CHUNK]) for u in range(2)]
        x1 = [small(f"x1{u}", [P, D]) for u in range(2)]
        row = [small(f"row{u}", [P, ROW]) for u in range(2)]
        zeros = at("zeros", o, [P, D], F32)
        slot_in_tile = small("slot_in_tile", [P, TILES * TOP, P], F16)
        ident = small("ident", [P, P])
        before = small("before", [P, P], BF16)
        ones = small("ones", [P, P], BF16)
        iota_p = small("iota_p", [P, P], F16)
        one_row = small("one_row", [1, P])
        rb = small("rb", [1, E])
        rw = small("rw", [P, DC, E])
        iota_e = small("iota_e", [P, E])
        iota_j = small("iota_j", [P, SLOT_TILES])
        earlier = small("earlier", [P, E, E])
        token_1 = small("token_1", [P, TILES])
        pad_off = small("pad_off", [P, TILES])
        dump = small("dump", [P, 1])
        half = small("half", [P, 2])
        half_dinv = small("half_dinv", [P, TILES])
        chosen_all = small("chosen_all", [P, TILES, TOP, E], BF16)
        tile_rank = small("tile_rank", [P, TILES, TOP])
        stats = small("stats", [P, 6])
        mv = [small(f"mv{u}", [P, 2]) for u in range(2)]
        row_sum = small("row_sum", [P, 1])
        deg = small("deg", [P, 1])
        positive = small("positive", [P, 1])
        pow_in = [small(f"pow_in{u}", [P, 2]) for u in range(2)]
        pow_out = [small(f"pow_out{u}", [P, 2]) for u in range(2)]
        y_scale = small("y_scale", [P, 1])
        top_logits = small("top_logits", [P, 8])
        neg_max = small("neg_max", [P, 1])
        exps = small("exps", [P, E])
        exp_sum = small("exp_sum", [P, 1])
        inv_sum = small("inv_sum", [P, 1])
        probs = small("probs", [P, E])
        top = small("top", [P, 8])
        top_at = small("top_at", [P, 8], U32)
        pair_sum = small("pair_sum", [P, 1])
        inv_pair = small("inv_pair", [P, 1])
        gate = small("gate", [P, TOP])
        expert = small("expert", [P, TOP])
        chosen = small("chosen", [P, TOP, E])
        gates = small("gates", [P, E])
        count = small("count", [P, E], BF16)
        counts = small("counts", [P, E], BF16)
        ranks = small("ranks", [P, TOP, E])
        rank = small("rank", [P, TOP])
        rank_i = small("rank_i", [P, TOP], I32)
        in_tile_i = small("in_tile_i", [P, TOP], I32)
        in_tile = small("in_tile", [P, TOP])
        total_i = small("total_i", [P, E], I32)
        size_i = small("size_i", [P, E], I32)
        size = small("size", [P, E])
        first = small("first", [P, E])
        end = small("end", [P, E])
        tile_of = small("tile_of", [P, TILES * TOP])
        expert_f = small("expert_f", [1, SLOT_TILES])
        expert_of = small("expert_of", [1, SLOT_TILES], I32)
        from_row = small("from_row", [P, SLOT_TILES], U32)
        to_row = small("to_row", [P, SLOT_TILES], U32)
        from_now = [small(f"from_now{u}", [P, 1], U32) for u in range(2)]
        to_now = small("to_now", [P, 1], U32)
        slot_gate = small("slot_gate", [P, SLOT_TILES])

        bank = [ctx.enter_context(nc.psum_tensor(f"bank{b}", [P, 512], F32)) for b in range(8)]
        z_bank = [bank[i] if i < STREAM else bank[(7, 0, 1, 2)[i - STREAM]] for i in range(TILES)]
        x1_bank = [bank[3], bank[4]]
        turn_bank = bank[5]
        logits = bank[6][:, 0:E]
        rank_ps = bank[6][:, 64:64 + E]
        total_ps = bank[6][:, 128:128 + E]
        token_ps = bank[6][:, 192:192 + SLOT_TILES]
        xt_bank, h_bank, ht_bank, y_bank = bank[0:2], bank[2:4], bank[4:6], bank[6:8]

        rows_dram = nc.dram_tensor("rows_dram", [NP, ROW], F32, kind="Internal").ap()

        zeros_ready = sem("zeros_ready")
        consts = sem("consts")
        small_in = sem("small_in")
        adj_in = sems("adj_in")
        deg_ready = sem("deg_ready")
        inv_ready = sem("inv_ready")
        sum_ready = sem("sum_ready")
        y_ready = sem("y_ready")
        stream_hi_ready = sem("stream_hi_ready")
        keep_hi_ready = sem("keep_hi_ready")
        y_hi_ready = sem("y_hi_ready")
        stream_lo_ready = sem("stream_lo_ready")
        keep_lo_ready = sem("keep_lo_ready")
        y_lo_ready = sem("y_lo_ready")
        stream_used = sem("stream_used")
        z_done = sem("z_done")
        z_hi_ready = sem("z_hi_ready")
        z_lo_ready = sem("z_lo_ready")
        col_in = sems("col_in")
        x_in = sems("x_in")
        col_hi_ready = sem("col_hi_ready")
        col_lo_ready = sem("col_lo_ready")
        col_used = sem("col_used")
        x1_ready = sem("x1_ready")
        x1_stored = sems("x1_stored")
        var_ready = sem("var_ready")
        rstd_ready = sem("rstd_ready")
        xn_ready = sem("xn_ready")
        turned = sem("turned")
        xn_t_ready = sem("xn_t_ready")
        logits_done = sem("logits_done")
        max_ready = sem("max_ready")
        exp_ready = sem("exp_ready")
        row_ready = sem("row_ready")
        row_stored = sems("row_stored")
        count_ready = sem("count_ready")
        rank_done = sem("rank_done")
        slots_ready = sem("slots_ready")
        chunk_in = sems("chunk_in")
        chunk_hi_ready = sem("chunk_hi_ready")
        chunk_lo_ready = sem("chunk_lo_ready")
        bias_in = sem("bias_in")
        dump_stored = sem("dump_stored")
        total_done = sem("total_done")
        place_ready = sem("place_ready")
        token_done = sem("token_done")
        index_ready = sem("index_ready")
        from_set = sem("from_set")
        to_set = sem("to_set")
        gathered = sems("gathered")
        xt_done = sem("xt_done")
        xt_hi_ready = sem("xt_hi_ready")
        xt_lo_ready = sem("xt_lo_ready")
        gate_ready = sem("gate_ready")
        h_done = sem("h_done")
        h_sum_ready = sem("h_sum_ready")
        h_ready = sem("h_ready")
        ht_done = sem("ht_done")
        ht_hi_ready = sem("ht_hi_ready")
        ht_lo_ready = sem("ht_lo_ready")
        y_done = sem("y_done")
        y_sum_ready = sem("y_sum_ready")
        y_out_ready = sem("y_out_ready")
        added = sem("added")
        dve_step = sem("dve_step")
        dve_passed = sem("dve_passed")
        pool_passed = sem("pool_passed")
        pool_step = sem("pool_step")

        def over(eng, count, peeled, looped, step):
            def straight(n):
                step(n, n % 2, n // 2 + 1)

            for n in range(peeled):
                straight(n)
            with eng.Fori(0, looped // 2) as turn:
                for v in range(2):
                    n = peeled + v
                    step(turn * 2 + n, n % 2, turn + n // 2 + 1)
            for n in range(peeled + looped, count):
                straight(n)

        def over_tiles(eng, step):
            over(eng, TILES, 3, TILES - 3, step)

        def over_slots(eng, step):
            over(eng, SLOT_TILES + 3, 5, (SLOT_TILES - 5) // 2 * 2, step)


        def works(n, lag):
            return not isinstance(n, int) or 0 <= n - lag < SLOT_TILES

        def w1(part, e, c):
            return part[:, :, :].rearrange("p n c -> p (n c)")[:, ds(e * (DC * FE) + c * FE, FE)]

        def w2(part, e, c):
            return part[:, :, :].rearrange("p n c -> p (n c)")[
                :, ds(e * (FC * D) + (W2_CHUNK * CHUNK + c * D), D)]

        block = ctx.enter_context(nc.Block())

        @block.sync
        def _(sp):
            sp.dma_start(rw[:, :, :], router_w).then_inc(small_in, 16)
            sp.dma_start(rb[:, :], router_b).then_inc(small_in, 16)

            def load_rows(k, u, use):
                if not isinstance(k, int) or k >= 2:
                    sp.wait_ge(y_ready, k - 1)
                    sp.wait_ge(sum_ready, k - 1)
                sp.dma_start(x_row[u][:, :], x_rows[ds(k * P, P), :]).then_inc(adj_in[u], 16)
                sp.dma_start(a_row[u][:, :], adj_rows[ds(k * P, P), :]).then_inc(adj_in[u], 16)
                sp.dma_start(at_row[u][:, :], adjt_rows[ds(k * P, P), :]).then_inc(adj_in[u], 16)

            over_tiles(sp, load_rows)

            def load_col(i, u):
                sp.dma_start(col[u][:, :], adjt_cols[ds(i * P, P), :]).then_inc(col_in[u], 16)

            def load_x(i, u):
                sp.dma_start(x1[u][:, :], x_rows[ds(i * P, P), :]).then_inc(x_in[u], 16)

            def load_chunk(c, u):
                if not isinstance(c, int) or c >= 2:
                    sp.wait_ge(chunk_lo_ready, c - 1)
                sp.dma_start(chunk[u][:, :], weights[ds(c * P, P), :]).then_inc(chunk_in[u], 16)

            sp.wait_ge(zeros_ready, 1)
            sp.dma_start(out[N:OUT_ROWS, :], zeros[:, :]).then_inc(dump_stored, 16)
            sp.wait_ge(sum_ready, TILES)
            for i in range(2):
                load_x(i, i)
                load_col(i, i)

            def store_tile(i, u, rows=P):
                sp.wait_ge(x1_ready, i + 1)
                sp.dma_start(out[ds(i * P, rows), :], x1[u][0:rows, :]).then_inc(x1_stored[u], 16)
                sp.wait_ge(row_ready, i + 1)
                sp.dma_start(rows_dram[ds(i * P, P), :], row[u][:, :]).then_inc(row_stored[u], 16)

            def serve_tile(i, u, use):
                sp.wait_ge(col_lo_ready, i + 1)
                load_col(i + 2, u)
                load_chunk(2 * i, 0)
                load_chunk(2 * i + 1, 1)
                store_tile(i, u)
                sp.wait_ge(x1_stored[u], 16 * use)
                load_x(i + 2, u)

            over(sp, TILES - 2, 3, TILES - 5, serve_tile)
            for i in range(TILES - 2, TILES):
                load_chunk(2 * i, 0)
                load_chunk(2 * i + 1, 1)
                store_tile(i, i % 2, P if i < TILES - 1 else LAST)
            with sp.Fori(0, (CHUNKS - EARLY) // 2) as t:
                load_chunk(t * 2 + EARLY, 0)
                load_chunk(t * 2 + (EARLY + 1), 1)
            sp.wait_ge(col_used, TILES)
            sp.dma_start(b1_all[:, :], b1.broadcast_to([P, E * FE])).then_inc(bias_in, 16)
            sp.dma_start(b2_all[:, :], b2.broadcast_to([P, E * D])).then_inc(bias_in, 16)

        @block.gpsimd
        def _(pool):
            pool.memset(zeros[:, :], 0.0).then_inc(zeros_ready, 1)
            pool.memset(half[:, :], -0.5).then_inc(pool_step, 1)
            pool.memset(ident[:, :], 0.0).then_inc(pool_step, 1)
            pool.memset(before[:, :], 1.0).then_inc(pool_step, 1)
            pool.memset(earlier[:, :, :], 1.0).then_inc(pool_step, 1)
            pool.memset(pad_off[:, :], 0.0).then_inc(pool_step, 1)
            pool.memset(ones[:, :], 1.0).then_inc(pool_step, 1)
            pool.memset(one_row[:, :], 1.0).then_inc(pool_step, 1)
            pool.iota(iota_p[:, :], pattern=[[1, P]], base=0, channel_multiplier=0,
                      allow_small_or_imprecise_dtypes=True).then_inc(pool_step, 1)
            pool.iota(iota_e[:, :], pattern=[[1, E]], base=0, channel_multiplier=0,
                      allow_small_or_imprecise_dtypes=True).then_inc(pool_step, 1)
            pool.iota(iota_j[:, :], pattern=[[1, SLOT_TILES]], base=0, channel_multiplier=0,
                      allow_small_or_imprecise_dtypes=True).then_inc(pool_step, 1)
            pool.iota(token_1[:, :], pattern=[[P, TILES]], base=1, channel_multiplier=1,
                      allow_small_or_imprecise_dtypes=True).then_inc(pool_step, 1)
            pool.iota(dump[:, :], pattern=[[0, 1]], base=N + 1, channel_multiplier=1,
                      allow_small_or_imprecise_dtypes=True).then_inc(pool_step, 1)
            pool.wait_ge(pool_step, 12)
            pool.affine_select(out=ident[:, :], in_=ident[:, :], compare_op=ALU.not_equal, fill=1.0,
                               base=0, pattern=[[-1, P]], channel_multiplier=1).then_inc(consts, 1)
            pool.affine_select(out=before[:, :], in_=before[:, :], compare_op=ALU.is_gt, fill=0.0,
                               base=0, pattern=[[1, P]], channel_multiplier=-1).then_inc(consts, 1)
            pool.affine_select(out=earlier[:, :, :], in_=earlier[:, :, :], compare_op=ALU.is_gt, fill=0.0,
                               base=0, pattern=[[1, E], [-1, E]], channel_multiplier=0).then_inc(consts, 1)
            pool.affine_select(out=token_1[:, :], in_=token_1[:, :], compare_op=ALU.is_ge, fill=0.0,
                               base=N - 1, pattern=[[-P, TILES]], channel_multiplier=-1).then_inc(consts, 1)
            pool.affine_select(out=pad_off[:, :], in_=pad_off[:, :], compare_op=ALU.is_ge, fill=1000.0,
                               base=N - 1, pattern=[[-P, TILES]], channel_multiplier=-1).then_inc(consts, 1)

            def rows(k, u, use):
                pool.wait_ge(deg_ready, k + 1)
                pool.tensor_tensor(pow_out[u][:, :], pow_in[u][:, :], half[:, :], ALU.pow).then_inc(inv_ready, 1)
                pool.wait_ge(keep_hi_ready, k + 1)
                pool.tensor_tensor(keep_lo[:, ds(k, 1), :].rearrange("p k c -> p (k c)"),
                                   sum_row[u][:, SC:NP],
                                   keep_hi[:, ds(k, 1), :].rearrange("p k c -> p (k c)").bitcast(F32),
                                   ALU.subtract).then_inc(keep_lo_ready, 1)

            over_tiles(pool, rows)

            def split_col(i, u):
                pool.wait_ge(col_hi_ready, i + 1)
                pool.tensor_tensor(col_lo[u][:, :], col[u][:, :], col_hi[u][:, :].bitcast(F32),
                                   ALU.subtract).then_inc(col_lo_ready, 1)

            def split_chunk(c, u):
                pool.wait_ge(chunk_hi_ready, c + 1)
                pool.tensor_tensor(w_lo[:, ds(c, 1), :].rearrange("p k c -> p (k c)"), chunk[u][:, :],
                                   w_hi[:, ds(c, 1), :].rearrange("p k c -> p (k c)").bitcast(F32),
                                   ALU.subtract).then_inc(chunk_lo_ready, 1)

            def power(i, u):
                pool.wait_ge(var_ready, i + 1)
                pool.tensor_tensor(pow_out[u][:, 0:1], pow_in[u][:, 0:1], half[:, 0:1],
                                   ALU.pow).then_inc(rstd_ready, 1)

            pool.wait_ge(stream_lo_ready, TILES)
            pool.wait_ge(keep_lo_ready, TILES)
            split_col(0, 0)
            split_col(1, 1)
            pool.wait_ge(z_done, KEEP)

            def serve_tile(i, u, use, more=True):
                power(i, u)
                if more:
                    split_col(i + 2, u)
                split_chunk(i * 2, 0)
                split_chunk(i * 2 + 1, 1)

            over(pool, TILES - 2, 3, TILES - 5, serve_tile)
            for i in range(TILES - 2, TILES):
                serve_tile(i, i % 2, None, False)
            pool.wait_ge(col_used, TILES)
            with pool.Fori(0, (CHUNKS - EARLY) // 2) as t:
                split_chunk(t * 2 + EARLY, 0)
                split_chunk(t * 2 + (EARLY + 1), 1)

            pool.wait_ge(dump_stored, 16)
            pool.wait_ge(index_ready, 2)
            for u in range(2):
                pool.wait_ge(row_stored[u], 16 * ((TILES - u + 1) // 2))
                pool.wait_ge(x1_stored[u], 16 * ((TILES - u + 1) // 2))

            def slots(n, u, use):
                if works(n, 0):
                    if not isinstance(n, int) or n >= 2:
                        pool.wait_ge(xt_done, n - 1)
                        pool.wait_ge(gate_ready, n - 1)
                    pool.tensor_copy(from_now[u][:, :], from_row[:, ds(n, 1)]).then_inc(from_set, 1)
                    pool.wait_ge(from_set, n + 1)
                    pool.sem_inc(pool_passed, 1)
                    pool.indirect_dma_start(xg[u][:, :], None, rows_dram,
                                            bass.IndirectOffsetOnAxis(ap=from_now[u][:, :], axis=0)
                                            ).then_inc(gathered[u], 16)
                if works(n, 3):
                    pool.wait_ge(y_out_ready, n - 2)
                    if not isinstance(n, int) or n >= 4:
                        pool.wait_ge(added, 16 * (n - 3))
                    pool.tensor_copy(to_now[:, :], to_row[:, ds(n - 3, 1)]).then_inc(to_set, 1)
                    pool.wait_ge(to_set, n - 2)
                    pool.sem_inc(pool_passed, 1)
                    pool.indirect_dma_start(out, bass.IndirectOffsetOnAxis(ap=to_now[:, :], axis=0),
                                            y_out[1 - u][:, :], None, compute_op=ALU.add).then_inc(added, 16)

            over_slots(pool, slots)
            pool.wait_ge(added, 16 * SLOT_TILES)

        @block.scalar
        def _(act):
            def rows(k, u, use):
                act.wait_ge(sum_ready, k + 1)
                if not isinstance(k, int) or k >= 2:
                    act.wait_ge(stream_used, k - 1)
                act.activation(stream_hi[u][:, :], sum_row[u][:, 0:SC], ACT.Copy).then_inc(stream_hi_ready, 1)
                act.activation(keep_hi[:, ds(k, 1), :].rearrange("p k c -> p (k c)"), sum_row[u][:, SC:NP],
                               ACT.Copy).then_inc(keep_hi_ready, 1)
                act.wait_ge(y_ready, k + 1)
                act.activation(y_hi[:, ds(k, 1), :].rearrange("p k c -> p (k c)"), y_row[u][:, :],
                               ACT.Copy).then_inc(y_hi_ready, 1)

            over_tiles(act, rows)

            def split_col(i, u, use):
                act.wait_ge(col_in[u], 16 * use)
                if not isinstance(i, int) or i >= 2:
                    act.wait_ge(col_used, i - 1)
                act.activation(col_hi[u][:, :], col[u][:, :], ACT.Copy).then_inc(col_hi_ready, 1)

            def split_chunk(c, u, use):
                act.wait_ge(chunk_in[u], 16 * use)
                act.activation(w_hi[:, ds(c, 1), :].rearrange("p k c -> p (k c)"), chunk[u][:, :],
                               ACT.Copy).then_inc(chunk_hi_ready, 1)

            act.wait_ge(sum_ready, TILES)
            split_col(0, 0, 1)
            split_col(1, 1, 1)
            act.wait_ge(stream_used, TILES)
            for i in range(TILES):
                if i >= STREAM:
                    act.wait_ge(z_done, i + 1 - STREAM)
                act.activation(z_hi[:, i, :], z_bank[i][:, :], ACT.Copy,
                               scale=half_dinv[:, i:i + 1]).then_inc(z_hi_ready, 1)

            def serve_tile(i, u, use, more=True):
                if more:
                    split_col(i + 2, u, use + 1)
                act.wait_ge(turned, i + 1)
                act.activation(xn_t[:, :, :].rearrange("p c q -> p (c q)"), turn_bank[:, :],
                               ACT.Copy).then_inc(xn_t_ready, 1)
                act.wait_ge(max_ready, i + 1)
                act.activation(exps[:, :], logits, ACT.Exp, bias=neg_max[:, :],
                               accum_out=exp_sum[:, :]).then_inc(exp_ready, 1)
                split_chunk(i * 2, 0, i + 1)
                split_chunk(i * 2 + 1, 1, i + 1)

            over(act, TILES - 2, 3, TILES - 5, serve_tile)
            for i in range(TILES - 2, TILES):
                serve_tile(i, i % 2, i // 2 + 1, False)
            with act.Fori(0, (CHUNKS - EARLY) // 2) as t:
                split_chunk(t * 2 + EARLY, 0, t + (EARLY // 2 + 1))
                split_chunk(t * 2 + (EARLY + 1), 1, t + (EARLY // 2 + 1))

            def slots(n, u, use):
                v = 1 - u
                if works(n, 0):
                    act.wait_ge(xt_done, n + 1)
                    if not isinstance(n, int) or n >= 2:
                        act.wait_ge(h_done, n - 1)
                    act.activation(xt_hi[u][:, :], xt_bank[u][:, :], ACT.Copy).then_inc(xt_hi_ready, 1)
                if works(n, 1):
                    act.wait_ge(h_sum_ready, n)
                    if not isinstance(n, int) or n >= 3:
                        act.wait_ge(ht_done, n - 2)
                    act.activation(h_act[v][:, :], h_sum[v][:, :], ACT.Gelu).then_inc(h_ready, 1)
                if works(n, 2):
                    act.wait_ge(ht_done, n - 1)
                    if not isinstance(n, int) or n >= 4:
                        act.wait_ge(y_done, n - 3)
                    act.activation(ht_hi[u][:, :], ht_bank[u][:, 0:FE], ACT.Copy).then_inc(ht_hi_ready, 1)
                if works(n, 3):
                    act.wait_ge(y_sum_ready, n - 2)
                    if not isinstance(n, int) or n >= 5:
                        act.wait_ge(added, 16 * (n - 4))
                    act.activation(y_out[v][:, :], y_sum[v][:, :], ACT.Copy,
                                   scale=slot_gate[:, ds(n - 3, 1)]).then_inc(y_out_ready, 1)

            over_slots(act, slots)

        @block.tensor
        def _(pe):
            def product(ps, hi, lo, rhs_hi, rhs_lo, start, stop):
                pe.matmul(ps, lo, rhs_hi, start=start, stop=False, skip_group_check=True)
                pe.matmul(ps, hi, rhs_lo, start=False, stop=False, skip_group_check=True)
                return pe.matmul(ps, hi, rhs_hi, start=False, stop=stop, skip_group_check=True)

            def y_at(part, k):
                return part[:, ds(k, 1), :].rearrange("p k c -> p (k c)")

            def rows(k, u, use):
                pe.wait_ge(y_lo_ready, k + 1)
                pe.wait_ge(stream_lo_ready, k + 1)
                for i in range(STREAM):
                    last = product(bank[i][:, :], stream_hi[u][:, i * P:(i + 1) * P],
                                   stream_lo[u][:, i * P:(i + 1) * P], y_at(y_hi, k), y_at(y_lo, k),
                                   isinstance(k, int) and k == 0, True)
                last.then_inc(stream_used, 1)

            over_tiles(pe, rows)
            pe.wait_ge(keep_lo_ready, TILES)
            for i in range(KEEP):
                if i:
                    pe.wait_ge(z_lo_ready, i)
                for k in range(TILES):
                    last = product(z_bank[STREAM + i][:, :], keep_hi[:, k, i * P:(i + 1) * P],
                                   keep_lo[:, k, i * P:(i + 1) * P], y_hi[:, k, :], y_lo[:, k, :],
                                   k == 0, k == TILES - 1)
                last.then_inc(z_done, 1)

            def turn(i, u):
                pe.wait_ge(xn_ready, i + 1)
                if not isinstance(i, int) or i >= 1:
                    pe.wait_ge(xn_t_ready, i)
                for c in range(DC):
                    last = pe.transpose(turn_bank[:, c * P:(c + 1) * P], row[u][:, c * P:(c + 1) * P], ident[:, :])
                last.then_inc(turned, 1)

            def route(i):
                pe.wait_ge(xn_t_ready, i + 1)
                pe.matmul(logits, one_row[:, :], rb[:, :], start=True, stop=False)
                for c in range(DC):
                    last = pe.matmul(logits, xn_t[:, c, :], rw[:, c, :], start=False, stop=c == DC - 1)
                last.then_inc(logits_done, 1)

            def rank_of(i):
                pe.wait_ge(count_ready, i + 1)
                pe.matmul(rank_ps, before[:, :], count[:, :], start=True, stop=False)
                pe.matmul(rank_ps, ones[:, :], counts[:, :], start=False, stop=True).then_inc(rank_done, 1)

            def columns(i, u, use):
                pe.wait_ge(col_lo_ready, i + 1)
                if not isinstance(i, int) or i >= 2:
                    pe.wait_ge(x1_ready, i - 1)
                for k in range(TILES):
                    if isinstance(i, int) and i == 0:
                        pe.wait_ge(z_lo_ready, max(k + 1, 5))
                    last = product(x1_bank[u][:, :], col_hi[u][:, k * P:(k + 1) * P],
                                   col_lo[u][:, k * P:(k + 1) * P], z_hi[:, k, :], z_lo[:, k, :],
                                   k == 0, k == TILES - 1)
                    if k == TILES - 1:
                        last.then_inc(col_used, 1)
                    if not isinstance(i, int) or i >= 1:
                        if k == 4:
                            turn(i - 1, 1 - u)
                        if k == 6:
                            route(i - 1)
                        if k == TILES - 1:
                            rank_of(i - 1)

            pe.wait_ge(small_in, 32)
            pe.wait_ge(consts, 5)
            over_tiles(pe, columns)
            turn(TILES - 1, 0)
            route(TILES - 1)
            rank_of(TILES - 1)
            pe.wait_ge(slots_ready, TILES)
            pe.matmul(total_ps, ones[:, :], counts[:, :], start=True, stop=True).then_inc(total_done, 1)
            pe.wait_ge(place_ready, 1)
            for m in range(TILES * TOP):
                last = pe.matmul(token_ps, slot_in_tile[:, m, :], slot_token[:, m, :],
                                 start=m == 0, stop=m == TILES * TOP - 1)
            last.then_inc(token_done, 1)

            def slots(n, u, use):
                v = 1 - u
                if works(n, 0):
                    pe.wait_ge(gathered[u], 16 * use)
                    if not isinstance(n, int) or n >= 2:
                        pe.wait_ge(xt_lo_ready, n - 1)
                    for c in range(DC):
                        last = pe.transpose(xt_bank[u][:, c * P:(c + 1) * P], xg[u][:, c * P:(c + 1) * P],
                                            ident[:, :])
                    last.then_inc(xt_done, 1)
                if works(n, 1):
                    e = pe.value_load(expert_of[0:1, ds(n - 1, 1)], min_val=0, max_val=E - 1)
                    pe.wait_ge(xt_lo_ready, n)
                    if not isinstance(n, int) or n >= 3:
                        pe.wait_ge(h_sum_ready, n - 2)
                    for c in range(DC):
                        last = product(h_bank[v][:, 0:FE], xt_hi[v][:, c * P:(c + 1) * P],
                                       xt_lo[v][:, c * P:(c + 1) * P], w1(w_hi, e, c), w1(w_lo, e, c),
                                       c == 0, c == DC - 1)
                    last.then_inc(h_done, 1)
                if works(n, 2):
                    pe.wait_ge(h_ready, n - 1)
                    if not isinstance(n, int) or n >= 4:
                        pe.wait_ge(ht_lo_ready, n - 3)
                    for c in range(FC):
                        last = pe.transpose(ht_bank[u][:, c * P:(c + 1) * P], h_act[u][:, c * P:(c + 1) * P],
                                            ident[:, :])
                    last.then_inc(ht_done, 1)
                if works(n, 3):
                    e = pe.value_load(expert_of[0:1, ds(n - 3, 1)], min_val=0, max_val=E - 1)
                    pe.wait_ge(ht_lo_ready, n - 2)
                    if not isinstance(n, int) or n >= 5:
                        pe.wait_ge(y_sum_ready, n - 4)
                    for c in range(FC):
                        last = product(y_bank[v][:, :], ht_hi[v][:, c * P:(c + 1) * P],
                                       ht_lo[v][:, c * P:(c + 1) * P], w2(w_hi, e, c), w2(w_lo, e, c),
                                       c == 0, c == FC - 1)
                    last.then_inc(y_done, 1)

            pe.wait_ge(index_ready, 2)
            pe.wait_ge(chunk_lo_ready, CHUNKS)
            over_slots(pe, slots)

        @block.vector
        def _(dve):
            class Steps:
                base = 0
                n = 0

                def then(self, ins, apart=False):
                    self.n += 1
                    ins.then_inc(dve_step, 1)
                    dve.wait_ge(dve_step, self.base + self.n)
                    if apart:
                        dve.sem_inc(dve_passed, 1)

            own = Steps()

            def counted(per_tile, step):
                start = own.base + own.n

                def one(k, u, use):
                    own.base, own.n = k * per_tile + start, 0
                    step(k, u, use)
                    assert own.n == per_tile, own.n

                over_tiles(dve, one)
                own.base, own.n = start + TILES * per_tile, 0

            def rows(k, u, use):
                dve.wait_ge(adj_in[u], 48 * use)
                own.then(dve.bn_stats(stats[:, :], x_row[u][:, :]), apart=True)
                own.then(dve.bn_aggr(mv[u][:, :], stats[:, :]))
                dve.tensor_scalar(pow_in[u][:, 1:2], mv[u][:, 1:2], EPS, None, ALU.add)
                if not isinstance(k, int) or k >= 2:
                    dve.wait_ge(keep_lo_ready, k - 1)
                    dve.sem_inc(dve_passed, 1)
                own.then(dve.tensor_tensor_reduce(sum_row[u][:, :], a_row[u][:, :], at_row[u][:, :], 1.0, 0.0,
                                                  ALU.add, ALU.add, row_sum[:, :]))
                own.then(dve.tensor_scalar(deg[:, :], row_sum[:, :], 0.5, 1.0, ALU.mult, ALU.add))
                dve.scalar_tensor_tensor(sum_row[u][:, ds(k * P, P)], ident[:, :], 2.0,
                                         sum_row[u][:, ds(k * P, P)], ALU.mult, ALU.add).then_inc(sum_ready, 1)
                dve.tensor_scalar(positive[:, :], deg[:, :], 0.0, None, ALU.is_gt)
                dve.tensor_scalar(pow_in[u][:, 0:1], deg[:, :], 1e-30, None, ALU.max).then_inc(deg_ready, 1)
                if not isinstance(k, int) or k >= 1:
                    low_parts(k - 1, 1 - u)
                dve.wait_ge(inv_ready, k + 1)
                dve.tensor_scalar(half_dinv[:, ds(k, 1)], pow_out[u][:, 0:1], positive[:, :], 0.5,
                                  ALU.mult, ALU.mult)
                own.then(dve.tensor_scalar(y_scale[:, :], pow_out[u][:, 0:1], positive[:, :],
                                           pow_out[u][:, 1:2], ALU.mult, ALU.mult))
                dve.tensor_scalar(y_row[u][:, :], x_row[u][:, :], mv[u][:, 0:1], y_scale[:, :],
                                  ALU.subtract, ALU.mult).then_inc(y_ready, 1)

            def low_parts(k, u):
                dve.wait_ge(stream_hi_ready, k + 1)
                dve.tensor_tensor(stream_lo[u][:, :], sum_row[u][:, 0:SC], stream_hi[u][:, :].bitcast(F32),
                                  ALU.subtract).then_inc(stream_lo_ready, 1)
                dve.wait_ge(y_hi_ready, k + 1)
                dve.tensor_tensor(y_lo[:, ds(k, 1), :].rearrange("p k c -> p (k c)"), y_row[u][:, :],
                                  y_hi[:, ds(k, 1), :].rearrange("p k c -> p (k c)").bitcast(F32),
                                  ALU.subtract).then_inc(y_lo_ready, 1)

            dve.wait_ge(consts, 5)
            counted(5, rows)
            low_parts(TILES - 1, 0)

            for i in range(TILES):
                dve.wait_ge(z_hi_ready, i + 1)
                dve.scalar_tensor_tensor(z_lo[:, i, :], z_bank[i][:, :], half_dinv[:, i:i + 1],
                                         z_hi[:, i, :].bitcast(F32), ALU.mult, ALU.subtract).then_inc(z_lo_ready, 1)

            own.then(dve.memset(counts[:, :], 0.0))
            dve.wait_ge(dump_stored, 16)

            def route_tile(i, u, use):
                if not isinstance(i, int) or i >= 2:
                    dve.wait_ge(row_stored[u], 16 * (use - 1))
                dve.wait_ge(x_in[u], 16 * use)
                dve.wait_ge(col_used, i + 1)
                dve.tensor_tensor(x1[u][:, :], x1_bank[u][:, :], x1[u][:, :], ALU.add).then_inc(x1_ready, 1)
                dve.wait_ge(x1_ready, i + 1)
                own.then(dve.bn_stats(stats[:, :], x1[u][:, :]), apart=True)
                own.then(dve.bn_aggr(mv[u][:, :], stats[:, :]))
                dve.tensor_scalar(pow_in[u][:, 0:1], mv[u][:, 1:2], EPS, None, ALU.add).then_inc(var_ready, 1)
                dve.wait_ge(rstd_ready, i + 1)
                dve.tensor_scalar(row[u][:, 0:D], x1[u][:, :], mv[u][:, 0:1], pow_out[u][:, 0:1],
                                  ALU.subtract, ALU.mult).then_inc(xn_ready, 1)
                dve.wait_ge(logits_done, i + 1)
                dve.sem_inc(dve_passed, 1)
                own.then(dve.max(top_logits[:, :], logits))
                dve.tensor_scalar(neg_max[:, :], top_logits[:, 0:1], -1.0, None, ALU.mult).then_inc(max_ready, 1)
                dve.wait_ge(exp_ready, i + 1)
                own.then(dve.reciprocal(inv_sum[:, :], exp_sum[:, :]))
                own.then(dve.tensor_scalar(probs[:, :], exps[:, :], inv_sum[:, :], None, ALU.mult), apart=True)
                own.then(dve.max(top[:, :], probs[:, :]), apart=True)
                own.then(dve.max_index(top_at[:, :], top[:, :], probs[:, :]))
                own.then(dve.tensor_tensor(pair_sum[:, :], top[:, 0:1], top[:, 1:2], ALU.add))
                own.then(dve.reciprocal(inv_pair[:, :], pair_sum[:, :]))
                dve.tensor_scalar(gate[:, :], top[:, 0:TOP], inv_pair[:, :], None, ALU.mult)
                own.then(dve.tensor_scalar(expert[:, :], top_at[:, 0:TOP], pad_off[:, ds(i, 1)], None, ALU.add))
                for c in range(TOP):
                    own.then(dve.tensor_scalar(chosen[:, c, :], iota_e[:, :], expert[:, c:c + 1], None,
                                               ALU.is_equal))
                own.then(dve.tensor_scalar(gates[:, :], chosen[:, 0, :], gate[:, 0:1], None, ALU.mult))
                dve.scalar_tensor_tensor(row[u][:, D:ROW], chosen[:, 1, :], gate[:, 1:2], gates[:, :],
                                         ALU.mult, ALU.add).then_inc(row_ready, 1)
                dve.tensor_tensor(count[:, :], chosen[:, 0, :], chosen[:, 1, :], ALU.add).then_inc(count_ready, 1)
                dve.tensor_copy(chosen_all[:, ds(i, 1), :, :].rearrange("p i t e -> p (i t e)"),
                                chosen[:, :, :].rearrange("p t e -> p (t e)"))
                dve.wait_ge(rank_done, i + 1)
                own.then(dve.tensor_tensor(ranks[:, :, :], chosen[:, :, :],
                                           rank_ps[:, None, :].broadcast_to([P, TOP, E]), ALU.mult))
                own.then(dve.tensor_reduce(rank[:, :], ranks[:, :, :], AX_X, ALU.add))
                own.then(dve.tensor_copy(rank_i[:, :], rank[:, :]))
                own.then(dve.tensor_scalar(in_tile_i[:, :], rank_i[:, :], P - 1, None, ALU.bitwise_and))
                own.then(dve.tensor_copy(in_tile[:, :], in_tile_i[:, :]))
                dve.tensor_tensor(tile_rank[:, ds(i, 1), :].rearrange("p i t -> p (i t)"), rank[:, :],
                                  in_tile[:, :], ALU.subtract)
                for c in range(TOP):
                    dve.tensor_scalar(slot_in_tile[:, ds(i * TOP + c, 1), :].rearrange("p i q -> p (i q)"),
                                      iota_p[:, :], in_tile[:, c:c + 1], None, ALU.is_equal)
                dve.tensor_tensor(counts[:, :], counts[:, :], count[:, :], ALU.add).then_inc(slots_ready, 1)

            counted(18, route_tile)

            dve.wait_ge(total_done, 1)
            own.then(dve.tensor_scalar(total_i[:, :], total_ps, float(P - 1), None, ALU.add))
            own.then(dve.tensor_scalar(size_i[:, :], total_i[:, :], 7, None, ALU.arith_shift_right))
            own.then(dve.tensor_copy(size[:, :], size_i[:, :]))
            own.then(dve.tensor_tensor(size_before[:, :, :], earlier[:, :, :],
                                       size[:, None, :].broadcast_to([P, E, E]), ALU.mult))
            own.then(dve.tensor_reduce(first[:, :], size_before[:, :, :], AX_X, ALU.add))
            dve.tensor_tensor(end[:, :], first[:, :], size[:, :], ALU.add)
            m = TILES * TOP
            own.then(dve.tensor_tensor(start_sel[:, :, :],
                                       chosen_all[:, :, :, :].rearrange("p i t e -> p (i t) e"),
                                       first[:, None, :].broadcast_to([P, m, E]), ALU.mult))
            own.then(dve.tensor_reduce(tile_of[:, :], start_sel[:, :, :], AX_X, ALU.add))
            own.then(dve.scalar_tensor_tensor(tile_of[:, :], tile_rank[:, :, :].rearrange("p i t -> p (i t)"),
                                              1.0 / P, tile_of[:, :], ALU.mult, ALU.add))
            own.then(dve.tensor_tensor(slot_place[:, :, :], iota_j[:, None, :].broadcast_to([P, m, SLOT_TILES]),
                                       tile_of[:, :, None].broadcast_to([P, m, SLOT_TILES]), ALU.is_equal))
            for c in range(TOP):
                last = dve.tensor_tensor(
                    slot_token[:, :, :].rearrange("p (i t) j -> p t i j", t=TOP)[:, c],
                    slot_place[:, :, :].rearrange("p (i t) j -> p t i j", t=TOP)[:, c],
                    token_1[:, :, None].broadcast_to([P, TILES, SLOT_TILES]), ALU.mult)
                if c == TOP - 1:
                    last.then_inc(place_ready, 1)
                else:
                    own.then(last)
            own.then(dve.tensor_tensor(over_j[:, :, :], end[0:1, None, :].broadcast_to([1, SLOT_TILES, E]),
                                       iota_j[0:1, :, None].broadcast_to([1, SLOT_TILES, E]), ALU.is_le))
            own.then(dve.tensor_reduce(expert_f[:, :], over_j[:, :, :], AX_X, ALU.add))
            dve.tensor_scalar(expert_of[:, :], expert_f[:, :], float(E - 1), None, ALU.min).then_inc(index_ready, 1)
            dve.wait_ge(token_done, 1)
            own.then(dve.tensor_scalar(token_0[:, :], token_ps, -1.0, None, ALU.add))
            own.then(dve.tensor_scalar(empty[:, :], token_ps, 0.0, None, ALU.is_equal))
            own.then(dve.tensor_scalar(from_row[:, :], token_0[:, :], 0.0, None, ALU.max))
            dve.scalar_tensor_tensor(to_row[:, :], empty[:, :], dump[:, :], token_0[:, :],
                                     ALU.mult, ALU.add).then_inc(index_ready, 1)
            dve.wait_ge(index_ready, 2)
            dve.wait_ge(bias_in, 32)

            def slots(n, u, use):
                v = 1 - u
                if works(n, 0):
                    dve.wait_ge(xt_hi_ready, n + 1)
                    dve.tensor_tensor(xt_lo[u][:, :], xt_bank[u][:, :], xt_hi[u][:, :].bitcast(F32),
                                      ALU.subtract).then_inc(xt_lo_ready, 1)
                    e = dve.value_load(expert_of[0:1, ds(n, 1)], min_val=0, max_val=E - 1)
                    dve.tensor_copy(slot_gate[:, ds(n, 1)], xg[u][:, ds(e + D, 1)]).then_inc(gate_ready, 1)
                if works(n, 1):
                    e = dve.value_load(expert_of[0:1, ds(n - 1, 1)], min_val=0, max_val=E - 1)
                    dve.wait_ge(h_done, n)
                    if not isinstance(n, int) or n >= 3:
                        dve.wait_ge(h_ready, n - 2)
                    dve.tensor_tensor(h_sum[v][:, :], h_bank[v][:, 0:FE], b1_all[:, ds(e * FE, FE)],
                                      ALU.add).then_inc(h_sum_ready, 1)
                if works(n, 2):
                    dve.wait_ge(ht_hi_ready, n - 1)
                    dve.tensor_tensor(ht_lo[u][:, :], ht_bank[u][:, 0:FE], ht_hi[u][:, :].bitcast(F32),
                                      ALU.subtract).then_inc(ht_lo_ready, 1)
                if works(n, 3):
                    e = dve.value_load(expert_of[0:1, ds(n - 3, 1)], min_val=0, max_val=E - 1)
                    dve.wait_ge(y_done, n - 2)
                    if not isinstance(n, int) or n >= 5:
                        dve.wait_ge(y_out_ready, n - 4)
                    dve.tensor_tensor(y_sum[v][:, :], y_bank[v][:, :], b2_all[:, ds(e * D, D)],
                                      ALU.add).then_inc(y_sum_ready, 1)

            over_slots(dve, slots)


_TENSORS = ["x_rows", "adj_rows", "adjt_rows", "adjt_cols", "weights", "router_w", "router_b", "b1", "b2"]


def kernel(x, adj, L0_ffn_router_w, L0_ffn_router_b, L0_ffn_W1, L0_ffn_b1, L0_ffn_W2, L0_ffn_b2):
    import numpy as np
    import concourse.bacc as bacc
    from concourse.bass_utils import run_bass_kernel_spmd

    adj_pad = np.pad(np.asarray(adj), ((0, NP - N), (0, NP - N)))
    adjt = np.ascontiguousarray(adj_pad.T)
    w1 = np.asarray(L0_ffn_W1).reshape(E, DC, P, FE).transpose(2, 0, 1, 3).reshape(P, W2_CHUNK, CHUNK)
    w2 = np.asarray(L0_ffn_W2).reshape(E, FC, P, D).transpose(2, 0, 1, 3).reshape(P, CHUNKS - W2_CHUNK, CHUNK)
    arrays = {
        "x_rows": np.pad(np.asarray(x), ((0, NP - N), (0, 0))),
        "adj_rows": adj_pad,
        "adjt_rows": adjt,
        "adjt_cols": adjt.reshape(TILES, P, TILES, P).transpose(2, 1, 0, 3).reshape(NP, NP),
        "weights": np.concatenate([w1, w2], 1).transpose(1, 0, 2).reshape(CHUNKS * P, CHUNK),
        "router_w": np.asarray(L0_ffn_router_w).reshape(DC, P, E).transpose(1, 0, 2),
        "router_b": np.asarray(L0_ffn_router_b).reshape(1, E),
        "b1": np.asarray(L0_ffn_b1).reshape(1, E * FE),
        "b2": np.asarray(L0_ffn_b2).reshape(1, E * D),
    }
    arrays = {n: np.ascontiguousarray(a) for n, a in arrays.items()}
    nc = bacc.Bacc("TRN2", target_bir_lowering=False, num_devices=1)
    args = [nc.dram_tensor(f"{n}_dram", arrays[n].shape, F32, kind="ExternalInput").ap() for n in _TENSORS]
    out = nc.dram_tensor("out_dram", [OUT_ROWS, D], F32, kind="ExternalOutput").ap()
    build(nc, *args, out)
    result = run_bass_kernel_spmd(nc, [{f"{n}_dram": a for n, a in arrays.items()}], core_ids=[0])
    return result.results[0]["out_dram"][:N]
```

```python
from contextlib import ExitStack

import concourse.bass as bass
from concourse import mybir

F32 = mybir.dt.float32
F32R = mybir.dt.float32r
F16 = mybir.dt.float16
BF16 = mybir.dt.bfloat16
I32 = mybir.dt.int32
U32 = mybir.dt.uint32
ALU = mybir.AluOpType
ACT = mybir.ActivationFunctionType
AX_X = mybir.AxisListType.X
ds = bass.ds

P = 128
N = 1354
D = 512
E = 8
FE = 256
TOP = 2
EPS = 1e-5
TILES = -(-N // P)
NP = TILES * P
DC = D // P
FC = FE // P
LAST = N - (TILES - 1) * P
SLOT_TILES = (TOP * N + E * (P - 1)) // P
ROW = D + E
STREAM = 7
KEEP = TILES - STREAM
GROUPS = (7, TILES - 7)
SC = STREAM * P
KC = KEEP * P
CHUNK = 512
W2_CHUNK = E * DC * FE // CHUNK
CHUNKS = W2_CHUNK + E * FC * D // CHUNK
EARLY = 22
ZERO_STORES = 16 * (1 + -(-(N + P) // P))
OUT_ROWS = N + P


def build(nc, x_rows, adj_rows, adjt_rows, adjt_cols, weights, router_w, router_b, b1, b2, out):
    with ExitStack() as ctx:
        base = -(-nc.sbuf_base // 32) * 32

        def at(name, offset, shape, dt):
            return nc.alloc_sbuf_tensor_at(name, shape, dt, offset=base + offset)

        def sem(name):
            return ctx.enter_context(nc.semaphore(name))

        def sems(name, n=2):
            return [sem(f"{name}{i}") for i in range(n)]

        ARENA = 212800
        ctx.enter_context(nc.sbuf_tensor("arena", [P, ARENA // 4], F32))
        w_hi = at("w_hi", 0, [P, CHUNKS, CHUNK], F32R)
        w_lo = at("w_lo", 65536, [P, CHUNKS, CHUNK], F32R)
        xn_t = at("xn_t", 4 * CHUNK * EARLY, [P, DC, P], F32)
        b1_all = at("b1_all", 131072, [P, E * FE], F32)
        b2_all = at("b2_all", 139264, [P, E * D], F32)
        y_hi = at("y_hi", 0, [P, TILES, D], F32R)
        y_lo = at("y_lo", 22528, [P, TILES, D], F32R)
        keep_hi = at("keep_hi", 45056, [P, TILES, KC], F32R)
        keep_lo = at("keep_lo", 67584, [P, TILES, KC], F32R)
        stream_hi = [at(f"stream_hi{u}", 90112 + 3584 * u, [P, SC], F32R) for u in range(2)]
        stream_lo = [at(f"stream_lo{u}", 97280 + 3584 * u, [P, SC], F32R) for u in range(2)]
        row_sum, deg, powers, dinv, plus_half = [
            at(name, 104448 + 32 * i, [P, n], F32) for i, (name, n) in enumerate(
                (("row_sum", 1), ("deg", 1), ("powers", 2), ("dinv", 1), ("plus_half", 1)))]
        positive = [at(f"positive{u}", 104640 + 32 * u, [P, 1], F32) for u in range(2)]
        y_scale = [at(f"y_scale{u}", 104704 + 32 * u, [P, 1], F32) for u in range(2)]
        power_in = [at(f"power_in{u}", 104768 + 32 * u, [P, 2], F32) for u in range(2)]
        ZB = 110592
        z_hi = at("z_hi", ZB, [P, TILES, D], F32R)
        z_lo = at("z_lo", ZB + 22528, [P, TILES, D], F32R)
        x_rows_in = at("x_rows_in", ZB, [P, TILES, D], F32)
        y_row = [at(f"y_row{u}", ZB + 22528 + 2048 * u, [P, D], F32) for u in range(2)]
        AB = 155648
        RB = 4 * NP
        a_row = [at(f"a_row{u}", AB + RB * u, [P, NP], F32) for u in range(2)]
        at_row = [at(f"at_row{u}", AB + RB * (2 + u), [P, NP], F32) for u in range(2)]
        sum_row = [at(f"sum_row{u}", AB + RB * (4 + u), [P, NP], F32) for u in range(2)]
        col = [at(f"col{u}", AB + RB * u, [P, NP], F32) for u in range(2)]
        col_hi = [at(f"col_hi{u}", AB + RB * (2 + u), [P, NP], F32R) for u in range(2)]
        col_lo = [at(f"col_lo{u}", AB + RB * (4 + u), [P, NP], F32R) for u in range(2)]
        o = AB

        def slot_buffer(name, cols, dt):
            nonlocal o
            both = [at(f"{name}{u}", o + 4 * cols * u, [P, cols], dt) for u in range(2)]
            o += 8 * cols
            return both

        xg = slot_buffer("xg", ROW, F32)
        xt_hi = slot_buffer("xt_hi", D, F32R)
        xt_lo = slot_buffer("xt_lo", D, F32R)
        h_sum = slot_buffer("h_sum", FE, F32)
        h_act = slot_buffer("h_act", FE, F32)
        ht_hi = slot_buffer("ht_hi", FE, F32R)
        ht_lo = slot_buffer("ht_lo", FE, F32R)
        y_sum = slot_buffer("y_sum", D, F32)
        y_out = slot_buffer("y_out", D, F32)

        def tail(name, shape, dt, advance=True):
            nonlocal o
            t = at(name, o, shape, dt)
            if advance:
                size = 2 if dt == F16 else 4
                for n in shape[1:]:
                    size *= n
                o += -(-size // 32) * 32
            assert o <= AB + 6 * RB
            return t

        slot_token = tail("slot_token", [P, TILES * TOP, SLOT_TILES], F16)
        start_sel = tail("start_sel", [P, TILES * TOP, E], F32, advance=False)
        over_j = tail("over_j", [1, SLOT_TILES, E], F32)
        size_before = tail("size_before", [P, E, E], F32)
        token_0 = tail("token_0", [P, SLOT_TILES], F32)
        empty = tail("empty", [P, SLOT_TILES], F32)
        from_row = tail("from_row", [P, SLOT_TILES], U32)
        to_row = tail("to_row", [P, SLOT_TILES], U32)
        expert_f = tail("expert_f", [1, SLOT_TILES], F32)
        expert_of = tail("expert_of", [1, SLOT_TILES], I32)
        slot_gate = tail("slot_gate", [P, SLOT_TILES], F32)
        tile_of = tail("tile_of", [P, TILES * TOP], F32)
        total_i = tail("total_i", [P, E], I32)
        size_i = tail("size_i", [P, E], I32)
        size = tail("size", [P, E], F32)
        first = tail("first", [P, E], F32)
        end = tail("end", [P, E], F32)
        o = AB + 6 * RB

        def small(name, shape, dt=F32):
            nonlocal o
            size = {F32: 4, F32R: 4, I32: 4, U32: 4, F16: 2, BF16: 2}[dt]
            for n in shape[1:]:
                size *= n
            t = at(name, o, shape, dt)
            o += -(-size // 32) * 32
            assert o <= ARENA
            return t

        chunk = [small(f"chunk{u}", [P, CHUNK]) for u in range(2)]
        x1 = [small(f"x1{u}", [P, D]) for u in range(2)]
        row = [small(f"row{u}", [P, D]) for u in range(2)]
        zeros = at("zeros", o, [P, D], F32)
        slot_in_tile = small("slot_in_tile", [P, TILES * TOP, P], F16)
        ident = small("ident", [P, P])
        before = small("before", [P, P], BF16)
        ones = small("ones", [P, P], BF16)
        iota_p = small("iota_p", [P, P], F16)
        rb = small("rb", [P, E])
        rw = small("rw", [P, DC, E])
        places_left = small("places_left", [P, E])
        iota_j = small("iota_j", [P, SLOT_TILES])
        earlier = small("earlier", [P, E, E])
        token_1 = small("token_1", [P, TILES])
        real = small("real", [P, TILES])
        dump = small("dump", [P, 1])
        half = small("half", [P, 2])
        half_dinv = small("half_dinv", [P, TILES])
        chosen = small("chosen", [P, TILES, TOP, E])
        count = small("count", [P, TILES, E], BF16)
        tile_rank = small("tile_rank", [P, TILES * TOP])
        logits_all = small("logits_all", [P, TILES, E])
        gates = small("gates", [P, TILES, E])
        G = GROUPS[0]
        probs = small("probs", [P, G, E])
        marks = small("marks", [P, G, E])
        ranks = small("ranks", [P, G * TOP, E])
        top = small("top", [P, TOP, G])
        first_of = small("first_of", [P, G])
        inv_sum = small("inv_sum", [P, G])
        rank = small("rank", [P, G * TOP])
        rank_i = small("rank_i", [P, G * TOP], I32)
        in_tile = small("in_tile", [P, G * TOP])
        stats = small("stats", [P, 6])
        mv = [small(f"mv{u}", [P, 2]) for u in range(2)]
        pow_in = [small(f"pow_in{u}", [P, 2]) for u in range(2)]
        pow_out = [small(f"pow_out{u}", [P, 2]) for u in range(2)]
        from_now = [small(f"from_now{u}", [P, 1], U32) for u in range(2)]
        to_now = [small(f"to_now{u}", [P, 1], U32) for u in range(2)]

        bank = [ctx.enter_context(nc.psum_tensor(f"bank{b}", [P, 512], F32)) for b in range(8)]
        z_bank = [bank[i] if i < STREAM else bank[(7, 0, 1, 2)[i - STREAM]] for i in range(TILES)]
        x1_bank = [bank[3], bank[4]]
        turn_bank = bank[5]
        logits = bank[6][:, 0:E]
        rank_ps = bank[7][:, 0:GROUPS[0] * E]
        total_ps = bank[6][:, 0:E]
        token_ps = bank[5][:, 0:SLOT_TILES]
        xt_bank, h_bank, ht_bank, y_bank = bank[0:2], bank[2:4], bank[4:6], bank[6:8]

        rows_dram = nc.dram_tensor("rows_dram", [NP, ROW], F32, kind="Internal").ap()
        odd_dram = nc.dram_tensor("odd_dram", [OUT_ROWS, D], F32, kind="Internal").ap()

        zeros_ready = sem("zeros_ready")
        consts = sem("consts")
        small_in = sem("small_in")
        adj_in = sems("adj_in")
        power_ready = sem("power_ready")
        scale_ready = sem("scale_ready")
        sum_ready = sem("sum_ready")
        half_ready = sem("half_ready")
        y_ready = sem("y_ready")
        stream_hi_ready = sem("stream_hi_ready")
        keep_hi_ready = sem("keep_hi_ready")
        y_hi_ready = sem("y_hi_ready")
        stream_lo_ready = sem("stream_lo_ready")
        keep_lo_ready = sem("keep_lo_ready")
        y_lo_ready = sem("y_lo_ready")
        stream_used = sem("stream_used")
        z_done = sem("z_done")
        z_hi_ready = sem("z_hi_ready")
        z_lo_ready = sem("z_lo_ready")
        col_in = sems("col_in")
        x_in = sems("x_in")
        col_hi_ready = sem("col_hi_ready")
        col_lo_ready = sem("col_lo_ready")
        col_lo2_ready = sem("col_lo2_ready")
        col_used = sem("col_used")
        x1_ready = sem("x1_ready")
        x1_stored = sems("x1_stored")
        var_ready = sem("var_ready")
        rstd_ready = sem("rstd_ready")
        xn_ready = sem("xn_ready")
        turned = sem("turned")
        xn_t_ready = sem("xn_t_ready")
        logits_done = sem("logits_done")
        logits_ready = sem("logits_ready")
        shifted = sem("shifted")
        exp_ready = sem("exp_ready")
        gates_ready = sem("gates_ready")
        gates_stored = sem("gates_stored")
        row_stored = sems("row_stored")
        count_ready = sem("count_ready")
        rank_done = sem("rank_done")
        slots_ready = sem("slots_ready")
        chunk_in = sems("chunk_in")
        chunk_hi_ready = sem("chunk_hi_ready")
        chunk_lo_ready = sem("chunk_lo_ready")
        bias_in = sem("bias_in")
        zeros_stored = sem("zeros_stored")
        total_done = sem("total_done")
        place_ready = sem("place_ready")
        token_done = sem("token_done")
        index_ready = sem("index_ready")
        from_set = sem("from_set")
        to_set = sem("to_set")
        gathered = sems("gathered")
        xt_done = sem("xt_done")
        xt_hi_ready = sem("xt_hi_ready")
        xt_lo_ready = sem("xt_lo_ready")
        gate_ready = sem("gate_ready")
        h_done = sem("h_done")
        h_sum_ready = sem("h_sum_ready")
        h_ready = sem("h_ready")
        ht_done = sem("ht_done")
        ht_hi_ready = sem("ht_hi_ready")
        ht_lo_ready = sem("ht_lo_ready")
        y_done = sem("y_done")
        y_sum_ready = sem("y_sum_ready")
        y_out_ready = sem("y_out_ready")
        added = sems("added")
        summed = sem("summed")
        dve_step = sem("dve_step")
        dve_passed = sem("dve_passed")
        pool_passed = sem("pool_passed")
        pool_step = sem("pool_step")

        def over(eng, count, peeled, looped, step):
            def straight(n):
                step(n, n % 2, n // 2 + 1)

            for n in range(peeled):
                straight(n)
            with eng.Fori(0, looped // 2) as turn:
                for v in range(2):
                    n = peeled + v
                    step(turn * 2 + n, n % 2, turn + n // 2 + 1)
            for n in range(peeled + looped, count):
                straight(n)

        def over_tiles(eng, step):
            over(eng, TILES, 3, TILES - 3, step)

        def over_slots(eng, step):
            over(eng, SLOT_TILES + 3, 5, (SLOT_TILES - 5) // 2 * 2, step)


        def works(n, lag):
            return not isinstance(n, int) or 0 <= n - lag < SLOT_TILES

        def w1(part, e, c):
            return part[:, :, :].rearrange("p n c -> p (n c)")[:, ds(e * (DC * FE) + c * FE, FE)]

        def w2(part, e, c):
            return part[:, :, :].rearrange("p n c -> p (n c)")[
                :, ds(e * (FC * D) + (W2_CHUNK * CHUNK + c * D), D)]

        block = ctx.enter_context(nc.Block())

        @block.sync
        def _(sp):
            def load_rows(k, u, use):
                if not isinstance(k, int) or k >= 2:
                    sp.wait_ge(sum_ready, k - 1)
                sp.dma_start(x_rows_in[:, ds(k, 1), :].rearrange("p k c -> p (k c)"),
                             x_rows[ds(k * P, P), :]).then_inc(adj_in[u], 16)
                sp.dma_start(a_row[u][:, :], adj_rows[ds(k * P, P), :]).then_inc(adj_in[u], 16)
                sp.dma_start(at_row[u][:, :], adjt_rows[ds(k * P, P), :]).then_inc(adj_in[u], 16)

            over_tiles(sp, load_rows)

            def load_col(i, u):
                sp.dma_start(col[u][:, :], adjt_cols[ds(i * P, P), :]).then_inc(col_in[u], 16)

            def load_x(i, u):
                sp.dma_start(x1[u][:, :], x_rows[ds(i * P, P), :]).then_inc(x_in[u], 16)

            def load_chunk(c, u):
                if not isinstance(c, int) or c >= 2:
                    sp.wait_ge(chunk_lo_ready, c - 1)
                sp.dma_start(chunk[u][:, :], weights[ds(c * P, P), :]).then_inc(chunk_in[u], 16)

            sp.dma_start(rw[:, :, :], router_w).then_inc(small_in, 16)
            sp.dma_start(rb[:, :], router_b.broadcast_to([P, E])).then_inc(small_in, 16)
            sp.wait_ge(sum_ready, TILES)
            for i in range(2):
                load_x(i, i)
                load_col(i, i)
            sp.wait_ge(zeros_ready, 1)
            sp.dma_start(out[N:OUT_ROWS, :], zeros[:, :]).then_inc(zeros_stored, 16)
            for r in range(0, OUT_ROWS, P):
                n = min(P, OUT_ROWS - r)
                sp.dma_start(odd_dram[r:r + n, :], zeros[0:n, :]).then_inc(zeros_stored, 16)

            def store_gates(g):
                a, b = sum(GROUPS[:g]), sum(GROUPS[:g + 1])
                sp.wait_ge(gates_ready, g + 1)
                sp.dma_start(rows_dram[a * P:b * P, D:ROW].rearrange("(i p) e -> p i e", p=P),
                             gates[:, a:b, :]).then_inc(gates_stored, 16)

            def store_tile(i, u, rows=P):
                sp.wait_ge(x1_ready, i + 1)
                sp.dma_start(out[ds(i * P, rows), :], x1[u][0:rows, :]).then_inc(x1_stored[u], 16)
                sp.wait_ge(xn_ready, i + 1)
                sp.dma_start(rows_dram[ds(i * P, P), 0:D], row[u][:, :]).then_inc(row_stored[u], 16)

            def serve_tile(i, u, use):
                sp.wait_ge(col_lo_ready, i + 1)
                sp.wait_ge(col_lo2_ready, i + 1)
                load_col(i + 2, u)
                load_chunk(i * 2, 0)
                load_chunk(i * 2 + 1, 1)
                store_tile(i, u)
                sp.wait_ge(x1_stored[u], 16 * use)
                load_x(i + 2, u)

            over(sp, TILES - 2, 3, TILES - 5, serve_tile)
            for i in range(TILES - 2, TILES):
                load_chunk(2 * i, 0)
                load_chunk(2 * i + 1, 1)
                store_tile(i, i % 2, P if i < TILES - 1 else LAST)
                if i == TILES - 2:
                    store_gates(0)
            with sp.Fori(0, (CHUNKS - EARLY) // 2) as t:
                load_chunk(t * 2 + EARLY, 0)
                load_chunk(t * 2 + (EARLY + 1), 1)
            sp.wait_ge(col_used, TILES)
            sp.dma_start(b1_all[:, :], b1.broadcast_to([P, E * FE])).then_inc(bias_in, 16)
            sp.dma_start(b2_all[:, :], b2.broadcast_to([P, E * D])).then_inc(bias_in, 16)
            store_gates(1)

        @block.gpsimd
        def _(pool):
            pool.memset(zeros[:, :], 0.0).then_inc(zeros_ready, 1)
            pool.memset(half[:, :], -0.5).then_inc(pool_step, 1)
            pool.memset(ident[:, :], 0.0).then_inc(pool_step, 1)
            pool.memset(before[:, :], 1.0).then_inc(pool_step, 1)
            pool.memset(earlier[:, :, :], 1.0).then_inc(pool_step, 1)
            pool.memset(real[:, :], 1.0).then_inc(pool_step, 1)
            pool.memset(ones[:, :], 1.0).then_inc(pool_step, 1)
            pool.iota(iota_p[:, :], pattern=[[1, P]], base=0, channel_multiplier=0,
                      allow_small_or_imprecise_dtypes=True).then_inc(pool_step, 1)
            pool.iota(places_left[:, :], pattern=[[-1, E]], base=E, channel_multiplier=0,
                      allow_small_or_imprecise_dtypes=True).then_inc(pool_step, 1)
            pool.iota(iota_j[:, :], pattern=[[1, SLOT_TILES]], base=0, channel_multiplier=0,
                      allow_small_or_imprecise_dtypes=True).then_inc(pool_step, 1)
            pool.iota(token_1[:, :], pattern=[[P, TILES]], base=1, channel_multiplier=1,
                      allow_small_or_imprecise_dtypes=True).then_inc(pool_step, 1)
            pool.iota(dump[:, :], pattern=[[0, 1]], base=N + 1, channel_multiplier=1,
                      allow_small_or_imprecise_dtypes=True).then_inc(pool_step, 1)
            pool.memset(plus_half[:, :], 0.5).then_inc(pool_step, 1)
            OWN = 12
            pool.wait_ge(pool_step, OWN)
            pool.affine_select(out=ident[:, :], in_=ident[:, :], compare_op=ALU.not_equal, fill=1.0,
                               base=0, pattern=[[-1, P]], channel_multiplier=1).then_inc(consts, 1)
            pool.affine_select(out=before[:, :], in_=before[:, :], compare_op=ALU.is_gt, fill=0.0,
                               base=0, pattern=[[1, P]], channel_multiplier=-1).then_inc(consts, 1)
            pool.affine_select(out=earlier[:, :, :], in_=earlier[:, :, :], compare_op=ALU.is_gt, fill=0.0,
                               base=0, pattern=[[1, E], [-1, E]], channel_multiplier=0).then_inc(consts, 1)
            pool.affine_select(out=token_1[:, :], in_=token_1[:, :], compare_op=ALU.is_ge, fill=0.0,
                               base=N - 1, pattern=[[-P, TILES]], channel_multiplier=-1).then_inc(consts, 1)
            pool.affine_select(out=real[:, :], in_=real[:, :], compare_op=ALU.is_ge, fill=0.0,
                               base=N - 1, pattern=[[-P, TILES]], channel_multiplier=-1).then_inc(consts, 1)

            def rows(k, u, use):
                before_tile = k * 2 + OWN
                pool.wait_ge(power_ready, k + 1)
                pool.tensor_tensor(powers[:, :], power_in[u][:, :], half[:, :], ALU.pow).then_inc(pool_step, 1)
                pool.wait_ge(pool_step, before_tile + 1)
                pool.tensor_tensor(dinv[:, :], powers[:, 0:1], positive[u][:, :], ALU.mult).then_inc(pool_step, 1)
                pool.wait_ge(pool_step, before_tile + 2)
                pool.tensor_tensor(y_scale[u][:, :], dinv[:, :], powers[:, 1:2], ALU.mult
                                   ).then_inc(scale_ready, 1)
                pool.tensor_tensor(half_dinv[:, ds(k, 1)], dinv[:, :], plus_half[:, :], ALU.mult
                                   ).then_inc(half_ready, 1)
                pool.wait_ge(keep_hi_ready, k + 1)
                pool.tensor_tensor(keep_lo[:, ds(k, 1), :].rearrange("p k c -> p (k c)"),
                                   sum_row[u][:, SC:NP],
                                   keep_hi[:, ds(k, 1), :].rearrange("p k c -> p (k c)").bitcast(F32),
                                   ALU.subtract).then_inc(keep_lo_ready, 1)
                pool.wait_ge(y_hi_ready, k + 1)
                pool.tensor_tensor(y_lo[:, ds(k, 1), :].rearrange("p k c -> p (k c)"), y_row[u][:, :],
                                   y_hi[:, ds(k, 1), :].rearrange("p k c -> p (k c)").bitcast(F32),
                                   ALU.subtract).then_inc(y_lo_ready, 1)

            over_tiles(pool, rows)

            def split_col(i, u):
                pool.wait_ge(col_hi_ready, i + 1)
                pool.tensor_tensor(col_lo[u][:, NP // 2:], col[u][:, NP // 2:],
                                   col_hi[u][:, NP // 2:].bitcast(F32), ALU.subtract).then_inc(col_lo_ready, 1)

            def split_chunk(c, u):
                pool.wait_ge(chunk_hi_ready, c + 1)
                pool.tensor_tensor(w_lo[:, ds(c, 1), :].rearrange("p k c -> p (k c)"), chunk[u][:, :],
                                   w_hi[:, ds(c, 1), :].rearrange("p k c -> p (k c)").bitcast(F32),
                                   ALU.subtract).then_inc(chunk_lo_ready, 1)

            def power(i, u):
                pool.wait_ge(var_ready, i + 1)
                pool.tensor_tensor(pow_out[u][:, 0:1], pow_in[u][:, 0:1], half[:, 0:1],
                                   ALU.pow).then_inc(rstd_ready, 1)

            pool.wait_ge(stream_lo_ready, TILES)
            pool.wait_ge(keep_lo_ready, TILES)
            split_col(0, 0)
            split_col(1, 1)
            pool.wait_ge(z_done, KEEP)

            def serve_tile(i, u, use, more=True):
                power(i, u)
                if more:
                    split_col(i + 2, u)
                split_chunk(i * 2, 0)
                split_chunk(i * 2 + 1, 1)

            over(pool, TILES - 2, 3, TILES - 5, serve_tile)
            for i in range(TILES - 2, TILES):
                serve_tile(i, i % 2, None, False)
            pool.wait_ge(col_used, TILES)
            with pool.Fori(0, (CHUNKS - EARLY) // 2) as t:
                split_chunk(t * 2 + EARLY, 0)
                split_chunk(t * 2 + (EARLY + 1), 1)

            pool.wait_ge(zeros_stored, ZERO_STORES)
            pool.wait_ge(index_ready, 2)
            pool.wait_ge(gates_stored, 32)
            for u in range(2):
                pool.wait_ge(row_stored[u], 16 * ((TILES - u + 1) // 2))
                pool.wait_ge(x1_stored[u], 16 * ((TILES - u + 1) // 2))

            def slots(n, u, use):
                if works(n, 0):
                    if not isinstance(n, int) or n >= 2:
                        pool.wait_ge(xt_done, n - 1)
                        pool.wait_ge(gate_ready, n - 1)
                    pool.tensor_copy(from_now[u][:, :], from_row[:, ds(n, 1)]).then_inc(from_set, 1)
                    pool.wait_ge(from_set, n + 1)
                    pool.sem_inc(pool_passed, 1)
                    pool.indirect_dma_start(xg[u][:, :], None, rows_dram,
                                            bass.IndirectOffsetOnAxis(ap=from_now[u][:, :], axis=0)
                                            ).then_inc(gathered[u], 16)
                if works(n, 6):
                    if not isinstance(n, int) or n >= 8:
                        pool.wait_ge(added[u], 16 * (use - 4))
                    pool.tensor_copy(to_now[u][:, :], to_row[:, ds(n - 6, 1)]).then_inc(to_set, 1)
                    pool.wait_ge(y_out_ready, n - 5)
                    pool.wait_ge(to_set, n - 5)
                    pool.sem_inc(pool_passed, 1)
                    pool.indirect_dma_start(odd_dram if u else out,
                                            bass.IndirectOffsetOnAxis(ap=to_now[u][:, :], axis=0),
                                            y_out[u][:, :], None, compute_op=ALU.add).then_inc(added[u], 16)

            over(pool, SLOT_TILES + 6, 9, (SLOT_TILES - 9) // 2 * 2, slots)
            for u in range(2):
                pool.wait_ge(added[u], 16 * ((SLOT_TILES - u + 1) // 2))
            pool.dma_start(out[0:N, :], odd_dram[0:N, :], accum_op=ALU.add, max_dma_last_dim=16 * D).then_inc(summed, 16)
            pool.wait_ge(summed, 16)

        @block.scalar
        def _(act):
            def rows(k, u, use):
                act.wait_ge(sum_ready, k + 1)
                if not isinstance(k, int) or k >= 2:
                    act.wait_ge(stream_used, k - 1)
                act.activation(stream_hi[u][:, :], sum_row[u][:, 0:SC], ACT.Copy).then_inc(stream_hi_ready, 1)
                act.activation(keep_hi[:, ds(k, 1), :].rearrange("p k c -> p (k c)"), sum_row[u][:, SC:NP],
                               ACT.Copy).then_inc(keep_hi_ready, 1)
                act.wait_ge(y_ready, k + 1)
                act.activation(y_hi[:, ds(k, 1), :].rearrange("p k c -> p (k c)"), y_row[u][:, :],
                               ACT.Copy).then_inc(y_hi_ready, 1)

            over_tiles(act, rows)

            def split_col(i, u, use):
                act.wait_ge(col_in[u], 16 * use)
                if not isinstance(i, int) or i >= 2:
                    act.wait_ge(col_used, i - 1)
                act.activation(col_hi[u][:, :], col[u][:, :], ACT.Copy).then_inc(col_hi_ready, 1)

            def split_chunk(c, u, use):
                act.wait_ge(chunk_in[u], 16 * use)
                act.activation(w_hi[:, ds(c, 1), :].rearrange("p k c -> p (k c)"), chunk[u][:, :],
                               ACT.Copy).then_inc(chunk_hi_ready, 1)

            act.wait_ge(sum_ready, TILES)
            split_col(0, 0, 1)
            split_col(1, 1, 1)
            act.wait_ge(half_ready, TILES)
            act.wait_ge(stream_used, TILES)
            for i in range(TILES):
                if i >= STREAM:
                    act.wait_ge(z_done, i + 1 - STREAM)
                act.activation(z_hi[:, i, :], z_bank[i][:, :], ACT.Copy,
                               scale=half_dinv[:, i:i + 1]).then_inc(z_hi_ready, 1)

            def serve_tile(i, u, use, more=True):
                if more:
                    split_col(i + 2, u, use + 1)
                act.wait_ge(turned, i + 1)
                act.activation(xn_t[:, :, :].rearrange("p c q -> p (c q)"), turn_bank[:, :],
                               ACT.Copy).then_inc(xn_t_ready, 1)
                split_chunk(i * 2, 0, i + 1)
                split_chunk(i * 2 + 1, 1, i + 1)

            def exponentials(g):
                act.wait_ge(shifted, g + 1)
                act.activation(probs[:, 0:GROUPS[g], :], probs[:, 0:GROUPS[g], :], ACT.Exp).then_inc(exp_ready, 1)

            over(act, TILES - 2, 3, TILES - 5, serve_tile)
            exponentials(0)
            for i in range(TILES - 2, TILES):
                serve_tile(i, i % 2, i // 2 + 1, False)
            exponentials(1)
            with act.Fori(0, (CHUNKS - EARLY) // 2) as t:
                split_chunk(t * 2 + EARLY, 0, t + (EARLY // 2 + 1))
                split_chunk(t * 2 + (EARLY + 1), 1, t + (EARLY // 2 + 1))

            def slots(n, u, use):
                v = 1 - u
                if works(n, 0):
                    act.wait_ge(xt_done, n + 1)
                    if not isinstance(n, int) or n >= 2:
                        act.wait_ge(h_done, n - 1)
                    act.activation(xt_hi[u][:, :], xt_bank[u][:, :], ACT.Copy).then_inc(xt_hi_ready, 1)
                if works(n, 1):
                    act.wait_ge(h_sum_ready, n)
                    if not isinstance(n, int) or n >= 3:
                        act.wait_ge(ht_done, n - 2)
                    act.activation(h_act[v][:, :], h_sum[v][:, :], ACT.Gelu).then_inc(h_ready, 1)
                if works(n, 2):
                    act.wait_ge(ht_done, n - 1)
                    if not isinstance(n, int) or n >= 4:
                        act.wait_ge(y_done, n - 3)
                    act.activation(ht_hi[u][:, :], ht_bank[u][:, 0:FE], ACT.Copy).then_inc(ht_hi_ready, 1)
                if works(n, 3):
                    act.wait_ge(y_sum_ready, n - 2)
                    if not isinstance(n, int) or n >= 5:
                        act.wait_ge(added[v], 16 * (use - 3 + u))
                    act.activation(y_out[v][:, :], y_sum[v][:, :], ACT.Copy,
                                   scale=slot_gate[:, ds(n - 3, 1)]).then_inc(y_out_ready, 1)

            over_slots(act, slots)

        @block.tensor
        def _(pe):
            def product(ps, hi, lo, rhs_hi, rhs_lo, start, stop):
                pe.matmul(ps, lo, rhs_hi, start=start, stop=False, skip_group_check=True)
                pe.matmul(ps, hi, rhs_lo, start=False, stop=False, skip_group_check=True)
                return pe.matmul(ps, hi, rhs_hi, start=False, stop=stop, skip_group_check=True)

            def y_at(part, k):
                return part[:, ds(k, 1), :].rearrange("p k c -> p (k c)")

            def rows(k, u, use):
                pe.wait_ge(y_lo_ready, k + 1)
                pe.wait_ge(stream_lo_ready, k + 1)
                for i in range(STREAM):
                    last = product(bank[i][:, :], stream_hi[u][:, i * P:(i + 1) * P],
                                   stream_lo[u][:, i * P:(i + 1) * P], y_at(y_hi, k), y_at(y_lo, k),
                                   isinstance(k, int) and k == 0, True)
                last.then_inc(stream_used, 1)

            over_tiles(pe, rows)
            pe.wait_ge(keep_lo_ready, TILES)
            for i in range(KEEP):
                if i:
                    pe.wait_ge(z_lo_ready, i)
                for k in range(TILES):
                    last = product(z_bank[STREAM + i][:, :], keep_hi[:, k, i * P:(i + 1) * P],
                                   keep_lo[:, k, i * P:(i + 1) * P], y_hi[:, k, :], y_lo[:, k, :],
                                   k == 0, k == TILES - 1)
                last.then_inc(z_done, 1)

            def turn(i, u):
                pe.wait_ge(xn_ready, i + 1)
                if not isinstance(i, int) or i >= 1:
                    pe.wait_ge(xn_t_ready, i)
                for c in range(DC):
                    last = pe.transpose(turn_bank[:, c * P:(c + 1) * P], row[u][:, c * P:(c + 1) * P], ident[:, :])
                last.then_inc(turned, 1)

            def route(i):
                pe.wait_ge(xn_t_ready, i + 1)
                if not isinstance(i, int) or i >= 1:
                    pe.wait_ge(logits_ready, i)
                for c in range(DC):
                    last = pe.matmul(logits, xn_t[:, c, :], rw[:, c, :], start=c == 0, stop=c == DC - 1)
                last.then_inc(logits_done, 1)

            def rank_group(g):
                a, b = sum(GROUPS[:g]), sum(GROUPS[:g + 1])
                pe.wait_ge(count_ready, g + 1)
                if g:
                    pe.wait_ge(slots_ready, g)
                pe.matmul(rank_ps[:, 0:(b - a) * E], before[:, :],
                          count[:, a:b, :].rearrange("p i e -> p (i e)"), start=True, stop=False)
                for i in range(b - 1):
                    at = max(i + 1, a)
                    last = pe.matmul(rank_ps[:, (at - a) * E:(b - a) * E], ones[:, :],
                                     count[:, i:i + 1, :].broadcast_to([P, b - at, E]),
                                     start=False, stop=i == b - 2)
                last.then_inc(rank_done, 1)

            def columns(i, u, use):
                pe.wait_ge(col_lo_ready, i + 1)
                pe.wait_ge(col_lo2_ready, i + 1)
                if not isinstance(i, int) or i >= 2:
                    pe.wait_ge(x1_ready, i - 1)
                for k in range(TILES):
                    if isinstance(i, int) and i == 0:
                        pe.wait_ge(z_lo_ready, max(k + 1, 5))
                    last = product(x1_bank[u][:, :], col_hi[u][:, k * P:(k + 1) * P],
                                   col_lo[u][:, k * P:(k + 1) * P], z_hi[:, k, :], z_lo[:, k, :],
                                   k == 0, k == TILES - 1)
                    if k == TILES - 1:
                        last.then_inc(col_used, 1)
                    if not isinstance(i, int) or i >= 1:
                        if k == 4:
                            turn(i - 1, 1 - u)
                        if k == 7:
                            route(i - 1)
                        if k == 3 and isinstance(i, int) and i == TILES - 1:
                            rank_group(0)

            pe.wait_ge(small_in, 32)
            pe.wait_ge(consts, 5)
            over(pe, TILES, 3, TILES - 5, columns)
            turn(TILES - 1, 0)
            route(TILES - 1)
            rank_group(1)
            for i in range(TILES):
                last = pe.matmul(total_ps, ones[:, :], count[:, i, :], start=i == 0, stop=i == TILES - 1)
            last.then_inc(total_done, 1)
            pe.wait_ge(place_ready, 1)
            for m in range(TILES * TOP):
                last = pe.matmul(token_ps, slot_in_tile[:, m, :], slot_token[:, m, :],
                                 start=m == 0, stop=m == TILES * TOP - 1)
            last.then_inc(token_done, 1)

            def slots(n, u, use):
                v = 1 - u
                if works(n, 0):
                    pe.wait_ge(gathered[u], 16 * use)
                    if not isinstance(n, int) or n >= 2:
                        pe.wait_ge(xt_lo_ready, n - 1)
                    for c in range(DC):
                        last = pe.transpose(xt_bank[u][:, c * P:(c + 1) * P], xg[u][:, c * P:(c + 1) * P],
                                            ident[:, :])
                    last.then_inc(xt_done, 1)
                if works(n, 1):
                    e = pe.value_load(expert_of[0:1, ds(n - 1, 1)], min_val=0, max_val=E - 1)
                    pe.wait_ge(xt_lo_ready, n)
                    if not isinstance(n, int) or n >= 3:
                        pe.wait_ge(h_sum_ready, n - 2)
                    for c in range(DC):
                        last = product(h_bank[v][:, 0:FE], xt_hi[v][:, c * P:(c + 1) * P],
                                       xt_lo[v][:, c * P:(c + 1) * P], w1(w_hi, e, c), w1(w_lo, e, c),
                                       c == 0, c == DC - 1)
                    last.then_inc(h_done, 1)
                if works(n, 2):
                    pe.wait_ge(h_ready, n - 1)
                    if not isinstance(n, int) or n >= 4:
                        pe.wait_ge(ht_lo_ready, n - 3)
                    for c in range(FC):
                        last = pe.transpose(ht_bank[u][:, c * P:(c + 1) * P], h_act[u][:, c * P:(c + 1) * P],
                                            ident[:, :])
                    last.then_inc(ht_done, 1)
                if works(n, 3):
                    e = pe.value_load(expert_of[0:1, ds(n - 3, 1)], min_val=0, max_val=E - 1)
                    pe.wait_ge(ht_lo_ready, n - 2)
                    if not isinstance(n, int) or n >= 5:
                        pe.wait_ge(y_sum_ready, n - 4)
                    else:
                        pe.wait_ge(chunk_lo_ready, CHUNKS)
                    for c in range(FC):
                        last = product(y_bank[v][:, :], ht_hi[v][:, c * P:(c + 1) * P],
                                       ht_lo[v][:, c * P:(c + 1) * P], w2(w_hi, e, c), w2(w_lo, e, c),
                                       c == 0, c == FC - 1)
                    last.then_inc(y_done, 1)

            pe.wait_ge(index_ready, 2)
            over_slots(pe, slots)

        @block.vector
        def _(dve):
            class Steps:
                base = 0
                n = 0

                def then(self, ins, apart=False):
                    self.n += 1
                    ins.then_inc(dve_step, 1)
                    dve.wait_ge(dve_step, self.base + self.n)
                    if apart:
                        dve.sem_inc(dve_passed, 1)

            own = Steps()

            def counted(per_tile, step, count, peeled, looped):
                start = own.base + own.n

                def one(k, u, use):
                    own.base, own.n = k * per_tile + start, 0
                    step(k, u, use)
                    assert own.n == per_tile, own.n

                over(dve, count, peeled, looped, one)
                own.base, own.n = start + count * per_tile, 0

            def rows(k, u, use):
                dve.wait_ge(adj_in[u], 48 * use)
                if not isinstance(k, int) or k >= 2:
                    dve.wait_ge(stream_lo_ready, k - 1)
                    dve.wait_ge(keep_lo_ready, k - 1)
                    dve.sem_inc(dve_passed, 1)
                own.then(dve.tensor_tensor_reduce(sum_row[u][:, :], a_row[u][:, :], at_row[u][:, :], 1.0, 0.0,
                                                  ALU.add, ALU.add, row_sum[:, :]))
                dve.scalar_tensor_tensor(sum_row[u][:, ds(k * P, P)], ident[:, :], 2.0,
                                         sum_row[u][:, ds(k * P, P)], ALU.mult, ALU.add).then_inc(sum_ready, 1)
                dve.tensor_scalar(deg[:, :], row_sum[:, :], 0.5, 1.0, ALU.mult, ALU.add).then_inc(dve_step, 1)
                own.n += 1
                own.then(dve.bn_stats(stats[:, :], x_at(k)), apart=True)
                dve.bn_aggr(mv[u][:, :], stats[:, :]).then_inc(dve_step, 1)
                own.n += 1
                dve.tensor_scalar(power_in[u][:, 0:1], deg[:, :], 1e-30, None, ALU.max).then_inc(dve_step, 1)
                own.n += 1
                own.then(dve.tensor_scalar(positive[u][:, :], deg[:, :], 0.0, None, ALU.is_gt))
                dve.tensor_scalar(power_in[u][:, 1:2], mv[u][:, 1:2], EPS, None, ALU.add).then_inc(power_ready, 1)
                if not isinstance(k, int) or k >= 1:
                    low_part(k - 1, 1 - u)
                dve.wait_ge(scale_ready, k + 1)
                if not isinstance(k, int) or k >= 2:
                    dve.wait_ge(y_lo_ready, k - 1)
                dve.tensor_scalar(y_row[u][:, :], x_at(k), mv[u][:, 0:1], y_scale[u][:, :],
                                  ALU.subtract, ALU.mult).then_inc(y_ready, 1)

            def x_at(k):
                return x_rows_in[:, ds(k, 1), :].rearrange("p k c -> p (k c)")

            def low_part(k, u):
                dve.wait_ge(stream_hi_ready, k + 1)
                dve.tensor_tensor(stream_lo[u][:, :], sum_row[u][:, 0:SC], stream_hi[u][:, :].bitcast(F32),
                                  ALU.subtract).then_inc(stream_lo_ready, 1)

            dve.wait_ge(consts, 5)
            counted(6, rows, TILES, 3, TILES - 3)
            low_part(TILES - 1, 0)

            def split_col(i, u):
                dve.wait_ge(col_hi_ready, i + 1)
                dve.tensor_tensor(col_lo[u][:, 0:NP // 2], col[u][:, 0:NP // 2],
                                  col_hi[u][:, 0:NP // 2].bitcast(F32), ALU.subtract).then_inc(col_lo2_ready, 1)

            dve.wait_ge(keep_lo_ready, TILES)
            dve.wait_ge(stream_lo_ready, TILES)
            split_col(0, 0)
            split_col(1, 1)
            for i in range(TILES):
                dve.wait_ge(z_hi_ready, i + 1)
                dve.scalar_tensor_tensor(z_lo[:, i, :], z_bank[i][:, :], half_dinv[:, i:i + 1],
                                         z_hi[:, i, :].bitcast(F32), ALU.mult, ALU.subtract).then_inc(z_lo_ready, 1)
            dve.wait_ge(small_in, 32)
            dve.wait_ge(zeros_stored, ZERO_STORES)

            def take_logits(i):
                dve.wait_ge(logits_done, i + 1)
                dve.tensor_tensor(logits_all[:, ds(i, 1), :].rearrange("p i e -> p (i e)"), logits, rb[:, :],
                                  ALU.add).then_inc(logits_ready, 1)

            def norm_tile(i, u, use, more=True):
                dve.wait_ge(x_in[u], 16 * use)
                dve.wait_ge(col_used, i + 1)
                dve.tensor_tensor(x1[u][:, :], x1_bank[u][:, :], x1[u][:, :], ALU.add).then_inc(x1_ready, 1)
                dve.wait_ge(x1_ready, i + 1)
                own.then(dve.bn_stats(stats[:, :], x1[u][:, :]), apart=True)
                own.then(dve.bn_aggr(mv[u][:, :], stats[:, :]))
                dve.tensor_scalar(pow_in[u][:, 0:1], mv[u][:, 1:2], EPS, None, ALU.add).then_inc(var_ready, 1)
                if not isinstance(i, int) or i >= 1:
                    take_logits(i - 1)
                if not isinstance(i, int) or i >= 2:
                    dve.wait_ge(row_stored[u], 16 * (use - 1))
                dve.wait_ge(rstd_ready, i + 1)
                dve.tensor_scalar(row[u][:, :], x1[u][:, :], mv[u][:, 0:1], pow_out[u][:, 0:1],
                                  ALU.subtract, ALU.mult).then_inc(xn_ready, 1)
                if more:
                    split_col(i + 2, u)

            def route_group(g):
                a, b = sum(GROUPS[:g]), sum(GROUPS[:g + 1])
                n = b - a
                pr, mk = probs[:, 0:n, :], marks[:, 0:n, :]
                firsts, inv = first_of[:, 0:n], inv_sum[:, 0:n]

                def wide(x):
                    return x[:, :, None].broadcast_to([P, n, E])

                dve.wait_ge(logits_ready, b)
                own.then(dve.tensor_reduce(firsts, logits_all[:, a:b, :], AX_X, ALU.max))
                dve.tensor_tensor(pr, logits_all[:, a:b, :], wide(firsts), ALU.subtract).then_inc(shifted, 1)
                dve.wait_ge(exp_ready, g + 1)
                own.then(dve.tensor_reduce(inv, pr, AX_X, ALU.add))
                own.then(dve.reciprocal(inv, inv))
                own.then(dve.tensor_tensor(pr, pr, wide(inv), ALU.mult))
                for c in range(TOP):
                    best = top[:, c, 0:n]
                    own.then(dve.tensor_reduce(best, pr, AX_X, ALU.max))
                    own.then(dve.tensor_tensor(mk, pr, wide(best), ALU.is_equal))
                    own.then(dve.tensor_tensor(mk, mk, places_left[:, None, :].broadcast_to([P, n, E]), ALU.mult))
                    own.then(dve.tensor_reduce(firsts, mk, AX_X, ALU.max))
                    own.then(dve.tensor_tensor(chosen[:, a:b, c, :], mk, wide(firsts), ALU.is_equal))
                    if c < TOP - 1:
                        own.then(dve.scalar_tensor_tensor(pr, chosen[:, a:b, c, :], -2.0, pr, ALU.mult, ALU.add))
                own.then(dve.tensor_tensor(inv, top[:, 0, 0:n], top[:, 1, 0:n], ALU.add))
                own.then(dve.reciprocal(inv, inv))
                own.then(dve.tensor_tensor(top[:, :, 0:n], top[:, :, 0:n],
                                           inv[:, None, :].broadcast_to([P, TOP, n]), ALU.mult))
                own.then(dve.tensor_tensor(mk, chosen[:, a:b, 0, :], wide(top[:, 0, 0:n]), ALU.mult))
                own.then(dve.tensor_tensor(pr, chosen[:, a:b, 1, :], wide(top[:, 1, 0:n]), ALU.mult))
                dve.tensor_tensor(gates[:, a:b, :], mk, pr, ALU.add).then_inc(gates_ready, 1)
                if b == TILES:
                    own.then(dve.tensor_tensor(
                        chosen[:, a:b, :, :].rearrange("p i t e -> p i (t e)"),
                        chosen[:, a:b, :, :].rearrange("p i t e -> p i (t e)"),
                        real[:, a:b, None].broadcast_to([P, n, TOP * E]), ALU.mult))
                dve.tensor_tensor(count[:, a:b, :], chosen[:, a:b, 0, :], chosen[:, a:b, 1, :],
                                  ALU.add).then_inc(count_ready, 1)

            def place_group(g):
                a, b = sum(GROUPS[:g]), sum(GROUPS[:g + 1])
                n, m = b - a, (b - a) * TOP
                dve.wait_ge(rank_done, g + 1)
                own.then(dve.tensor_tensor(
                    ranks[:, 0:m, :].rearrange("p (i t) e -> p i t e", t=TOP), chosen[:, a:b, :, :],
                    rank_ps[:, 0:n * E].rearrange("p (i e) -> p i e", e=E)[:, :, None, :].broadcast_to([P, n, TOP, E]),
                    ALU.mult))
                own.then(dve.tensor_reduce(rank[:, 0:m], ranks[:, 0:m, :], AX_X, ALU.add))
                own.then(dve.tensor_copy(rank_i[:, 0:m], rank[:, 0:m]))
                own.then(dve.tensor_scalar(rank_i[:, 0:m], rank_i[:, 0:m], P - 1, None, ALU.bitwise_and))
                own.then(dve.tensor_copy(in_tile[:, 0:m], rank_i[:, 0:m]))
                own.then(dve.tensor_tensor(tile_rank[:, a * TOP:b * TOP], rank[:, 0:m], in_tile[:, 0:m],
                                           ALU.subtract))
                for c in range(m):
                    last = dve.tensor_scalar(slot_in_tile[:, a * TOP + c, :], iota_p[:, :], in_tile[:, c:c + 1],
                                             None, ALU.is_equal)
                last.then_inc(slots_ready, 1)

            counted(2, norm_tile, TILES - 2, 3, TILES - 5)
            route_group(0)
            norm_tile(TILES - 2, 1, TILES // 2, False)
            place_group(0)
            norm_tile(TILES - 1, 0, TILES // 2 + 1, False)
            take_logits(TILES - 1)
            route_group(1)
            place_group(1)

            dve.wait_ge(total_done, 1)
            own.then(dve.tensor_scalar(total_i[:, :], total_ps, float(P - 1), None, ALU.add))
            own.then(dve.tensor_scalar(size_i[:, :], total_i[:, :], 7, None, ALU.arith_shift_right))
            own.then(dve.tensor_copy(size[:, :], size_i[:, :]))
            own.then(dve.tensor_tensor(size_before[:, :, :], earlier[:, :, :],
                                       size[:, None, :].broadcast_to([P, E, E]), ALU.mult))
            own.then(dve.tensor_reduce(first[:, :], size_before[:, :, :], AX_X, ALU.add))
            dve.tensor_tensor(end[:, :], first[:, :], size[:, :], ALU.add)
            m = TILES * TOP
            own.then(dve.tensor_tensor(start_sel[:, :, :],
                                       chosen[:, :, :, :].rearrange("p i t e -> p (i t) e"),
                                       first[:, None, :].broadcast_to([P, m, E]), ALU.mult))
            own.then(dve.tensor_reduce(tile_of[:, :], start_sel[:, :, :], AX_X, ALU.add))
            own.then(dve.scalar_tensor_tensor(tile_of[:, :], tile_rank[:, :],
                                              1.0 / P, tile_of[:, :], ALU.mult, ALU.add))
            own.then(dve.tensor_tensor(slot_token[:, :, :], iota_j[:, None, :].broadcast_to([P, m, SLOT_TILES]),
                                       tile_of[:, :, None].broadcast_to([P, m, SLOT_TILES]), ALU.is_equal))
            for c in range(TOP):
                part = slot_token[:, :, :].rearrange("p (i t) j -> p t i j", t=TOP)[:, c]
                last = dve.tensor_tensor(part, part, token_1[:, :, None].broadcast_to([P, TILES, SLOT_TILES]),
                                         ALU.mult)
            last.then_inc(place_ready, 1)
            own.then(dve.tensor_tensor(over_j[:, :, :], end[0:1, None, :].broadcast_to([1, SLOT_TILES, E]),
                                       iota_j[0:1, :, None].broadcast_to([1, SLOT_TILES, E]), ALU.is_le))
            own.then(dve.tensor_reduce(expert_f[:, :], over_j[:, :, :], AX_X, ALU.add))
            dve.tensor_scalar(expert_of[:, :], expert_f[:, :], float(E - 1), None, ALU.min).then_inc(index_ready, 1)
            dve.wait_ge(token_done, 1)
            own.then(dve.tensor_scalar(token_0[:, :], token_ps, -1.0, None, ALU.add))
            own.then(dve.tensor_scalar(empty[:, :], token_ps, 0.0, None, ALU.is_equal))
            own.then(dve.tensor_scalar(from_row[:, :], token_0[:, :], 0.0, None, ALU.max))
            dve.scalar_tensor_tensor(to_row[:, :], empty[:, :], dump[:, :], token_0[:, :],
                                     ALU.mult, ALU.add).then_inc(index_ready, 1)
            dve.wait_ge(index_ready, 2)
            dve.wait_ge(bias_in, 32)

            def slots(n, u, use):
                v = 1 - u
                if works(n, 0):
                    dve.wait_ge(xt_hi_ready, n + 1)
                    dve.tensor_tensor(xt_lo[u][:, :], xt_bank[u][:, :], xt_hi[u][:, :].bitcast(F32),
                                      ALU.subtract).then_inc(xt_lo_ready, 1)
                    e = dve.value_load(expert_of[0:1, ds(n, 1)], min_val=0, max_val=E - 1)
                    dve.tensor_copy(slot_gate[:, ds(n, 1)], xg[u][:, ds(e + D, 1)]).then_inc(gate_ready, 1)
                if works(n, 1):
                    e = dve.value_load(expert_of[0:1, ds(n - 1, 1)], min_val=0, max_val=E - 1)
                    dve.wait_ge(h_done, n)
                    if not isinstance(n, int) or n >= 3:
                        dve.wait_ge(h_ready, n - 2)
                    dve.tensor_tensor(h_sum[v][:, :], h_bank[v][:, 0:FE], b1_all[:, ds(e * FE, FE)],
                                      ALU.add).then_inc(h_sum_ready, 1)
                if works(n, 2):
                    dve.wait_ge(ht_hi_ready, n - 1)
                    dve.tensor_tensor(ht_lo[u][:, :], ht_bank[u][:, 0:FE], ht_hi[u][:, :].bitcast(F32),
                                      ALU.subtract).then_inc(ht_lo_ready, 1)
                if works(n, 3):
                    e = dve.value_load(expert_of[0:1, ds(n - 3, 1)], min_val=0, max_val=E - 1)
                    dve.wait_ge(y_done, n - 2)
                    if not isinstance(n, int) or n >= 5:
                        dve.wait_ge(y_out_ready, n - 4)
                    dve.tensor_tensor(y_sum[v][:, :], y_bank[v][:, :], b2_all[:, ds(e * D, D)],
                                      ALU.add).then_inc(y_sum_ready, 1)

            over_slots(dve, slots)


_TENSORS = ["x_rows", "adj_rows", "adjt_rows", "adjt_cols", "weights", "router_w", "router_b", "b1", "b2"]


def kernel(x, adj, L0_ffn_router_w, L0_ffn_router_b, L0_ffn_W1, L0_ffn_b1, L0_ffn_W2, L0_ffn_b2):
    import numpy as np
    import concourse.bacc as bacc
    from concourse.bass_utils import run_bass_kernel_spmd

    adj_pad = np.pad(np.asarray(adj), ((0, NP - N), (0, NP - N)))
    adjt = np.ascontiguousarray(adj_pad.T)
    w1 = np.asarray(L0_ffn_W1).reshape(E, DC, P, FE).transpose(2, 0, 1, 3).reshape(P, W2_CHUNK, CHUNK)
    w2 = np.asarray(L0_ffn_W2).reshape(E, FC, P, D).transpose(2, 0, 1, 3).reshape(P, CHUNKS - W2_CHUNK, CHUNK)
    arrays = {
        "x_rows": np.pad(np.asarray(x), ((0, NP - N), (0, 0))),
        "adj_rows": adj_pad,
        "adjt_rows": adjt,
        "adjt_cols": adjt.reshape(TILES, P, TILES, P).transpose(2, 1, 0, 3).reshape(NP, NP),
        "weights": np.concatenate([w1, w2], 1).transpose(1, 0, 2).reshape(CHUNKS * P, CHUNK),
        "router_w": np.asarray(L0_ffn_router_w).reshape(DC, P, E).transpose(1, 0, 2),
        "router_b": np.asarray(L0_ffn_router_b).reshape(1, E),
        "b1": np.asarray(L0_ffn_b1).reshape(1, E * FE),
        "b2": np.asarray(L0_ffn_b2).reshape(1, E * D),
    }
    arrays = {n: np.ascontiguousarray(a) for n, a in arrays.items()}
    nc = bacc.Bacc("TRN2", target_bir_lowering=False, num_devices=1)
    args = [nc.dram_tensor(f"{n}_dram", arrays[n].shape, F32, kind="ExternalInput").ap() for n in _TENSORS]
    out = nc.dram_tensor("out_dram", [OUT_ROWS, D], F32, kind="ExternalOutput").ap()
    build(nc, *args, out)
    result = run_bass_kernel_spmd(nc, [{f"{n}_dram": a for n, a in arrays.items()}], core_ids=[0])
    return result.results[0]["out_dram"][:N]
```

```python
from contextlib import ExitStack

import concourse.bass as bass
from concourse import mybir

F32 = mybir.dt.float32
F32R = mybir.dt.float32r
F16 = mybir.dt.float16
BF16 = mybir.dt.bfloat16
I32 = mybir.dt.int32
U32 = mybir.dt.uint32
ALU = mybir.AluOpType
ACT = mybir.ActivationFunctionType
AX_X = mybir.AxisListType.X
ds = bass.ds

P = 128
N = 1354
D = 512
E = 8
FE = 256
TOP = 2
EPS = 1e-5
TILES = -(-N // P)
NP = TILES * P
DC = D // P
FC = FE // P
LAST = N - (TILES - 1) * P
SLOT_TILES = (TOP * N + E * (P - 1)) // P
ROW = D + E
STREAM = 8
KEEP = TILES - STREAM
GROUPS = (7, TILES - 7)
SC = STREAM * P
KC = KEEP * P
LOW = 256
RANK_AT = (TILES - 1, 3)
A_TILES = (TOP * GROUPS[0] * P - E * (P - 1)) // P
assert A_TILES + (TOP * N - A_TILES * P + E * (P - 1)) // P == SLOT_TILES
CHUNK = 512
LAG = 6
PEELED = 9
assert PEELED >= max(A_TILES + 1, LAG + 3)
W2_CHUNK = E * DC * FE // CHUNK
CHUNKS = W2_CHUNK + E * FC * D // CHUNK
EARLY = 26
PER_TILE = 3
OUT_ROWS = N + P


def build(nc, x_rows, adj_rows, adjt_rows, adjt_cols, weights, router_w, router_b, b1, b2, out):
    with ExitStack() as ctx:
        base = -(-nc.sbuf_base // 32) * 32

        def at(name, offset, shape, dt):
            return nc.alloc_sbuf_tensor_at(name, shape, dt, offset=base + offset)

        def sem(name):
            return ctx.enter_context(nc.semaphore(name))

        def sems(name, n=2):
            return [sem(f"{name}{i}") for i in range(n)]

        ARENA = 212800
        ctx.enter_context(nc.sbuf_tensor("arena", [P, ARENA // 4], F32))
        w_parts = at("w_parts", 0, [P, CHUNKS, 2, CHUNK], F32R)
        xn_t = at("xn_t", 8 * CHUNK * EARLY, [P, DC, P], F32)
        b1_all = at("b1_all", 131072, [P, E * FE], F32)
        b2_all = at("b2_all", 139264, [P, E * D], F32)
        y_hi = at("y_hi", 0, [P, TILES, D], F32R)
        y_lo = at("y_lo", 22528, [P, TILES, D], F32R)
        keep_hi = at("keep_hi", 45056, [P, TILES, KC], F32R)
        keep_lo = at("keep_lo", 61952, [P, TILES, KC], F32R)
        stream_hi = [at(f"stream_hi{u}", 78848 + 4096 * u, [P, SC], F32R) for u in range(2)]
        stream_lo = [at(f"stream_lo{u}", 87040 + 4096 * u, [P, SC], F32R) for u in range(2)]
        row_sum, deg, powers, dinv, plus_half = [
            at(name, 104448 + 32 * i, [P, n], F32) for i, (name, n) in enumerate(
                (("row_sum", 1), ("deg", 1), ("powers", 2), ("dinv", 1), ("plus_half", 1)))]
        positive = [at(f"positive{u}", 104640 + 32 * u, [P, 1], F32) for u in range(2)]
        y_scale = [at(f"y_scale{u}", 104704 + 32 * u, [P, 1], F32) for u in range(2)]
        power_in = [at(f"power_in{u}", 104768 + 32 * u, [P, 2], F32) for u in range(2)]
        ZB = 110592
        z_hi = at("z_hi", ZB, [P, TILES, D], F32R)
        z_lo = at("z_lo", ZB + 22528, [P, TILES, D], F32R)
        x_rows_in = at("x_rows_in", ZB, [P, TILES, D], F32)
        x_less_mean = [at(f"x_less_mean{u}", ZB + 22528 + 2048 * u, [P, D], F32) for u in range(2)]
        AB = 155648
        RB = 4 * NP
        a_row = [at(f"a_row{u}", AB + RB * u, [P, NP], F32) for u in range(2)]
        at_row = [at(f"at_row{u}", AB + RB * (2 + u), [P, NP], F32) for u in range(2)]
        sum_row = [at(f"sum_row{u}", AB + RB * (4 + u), [P, NP], F32) for u in range(2)]
        col = [at(f"col{u}", AB + RB * u, [P, NP], F32) for u in range(2)]
        col_hi = [at(f"col_hi{u}", AB + RB * (2 + u), [P, NP], F32R) for u in range(2)]
        col_lo = [at(f"col_lo{u}", AB + RB * (4 + u), [P, NP], F32R) for u in range(2)]
        o = AB

        def slot_buffer(name, cols, dt):
            nonlocal o
            both = [at(f"{name}{u}", o + 4 * cols * u, [P, cols], dt) for u in range(2)]
            o += 8 * cols
            return both

        xg = slot_buffer("xg", ROW, F32)
        xt_hi = slot_buffer("xt_hi", D, F32R)
        xt_lo = slot_buffer("xt_lo", D, F32R)
        h_sum = slot_buffer("h_sum", FE, F32)
        h_act = slot_buffer("h_act", FE, F32)
        ht_hi = slot_buffer("ht_hi", FE, F32R)
        ht_lo = slot_buffer("ht_lo", FE, F32R)
        LATE_AT = o
        y_sum = slot_buffer("y_sum", D, F32)
        y_out = slot_buffer("y_out", D, F32)

        def tail(name, shape, dt, advance=True):
            nonlocal o
            t = at(name, o, shape, dt)
            if advance:
                size = 2 if dt == F16 else 4
                for n in shape[1:]:
                    size *= n
                o += -(-size // 32) * 32
            assert o <= AB + 6 * RB
            return t

        slot_token = [tail("slot_token0", [P, GROUPS[0] * TOP, A_TILES], F16),
                      tail("slot_token1", [P, TILES * TOP, SLOT_TILES - A_TILES], F16)]
        start_sel = tail("start_sel", [P, TILES * TOP, E], F32, advance=False)
        over_j = tail("over_j", [1, SLOT_TILES, E], F32)
        size_before = tail("size_before", [P, E, E], F32)
        token_0 = tail("token_0", [P, SLOT_TILES], F32)
        empty = tail("empty", [P, SLOT_TILES], F32)
        from_row = tail("from_row", [P, SLOT_TILES], U32)
        to_row = tail("to_row", [P, SLOT_TILES], U32)
        expert_f = tail("expert_f", [1, SLOT_TILES], F32)
        expert_of = tail("expert_of", [1, SLOT_TILES], I32)
        slot_gate = tail("slot_gate", [P, SLOT_TILES], F32)
        from_now = [tail(f"from_now{u}", [P, 1], U32) for u in range(2)]
        to_now = [tail(f"to_now{u}", [P, 1], U32) for u in range(2)]
        tile_of = tail("tile_of", [P, TILES * TOP], F32)
        limit = tail("limit", [P, TILES * TOP], F32)
        valid = tail("valid", [P, TILES * TOP], F32)
        total_i = tail("total_i", [P, E], I32)
        taken = tail("taken", [P, E], F32)
        shift = tail("shift", [P, E], F32)
        size_i = tail("size_i", [P, E], I32)
        size = tail("size", [P, E], F32)
        first = tail("first", [P, E], F32)
        end = tail("end", [P, E], F32)
        o = AB + 6 * RB

        def small(name, shape, dt=F32):
            nonlocal o
            size = {F32: 4, F32R: 4, I32: 4, U32: 4, F16: 2, BF16: 2}[dt]
            for n in shape[1:]:
                size *= n
            t = at(name, o, shape, dt)
            o += -(-size // 32) * 32
            assert o <= ARENA
            return t

        chunk = [small(f"chunk{u}", [P, CHUNK]) for u in range(2)]
        chunk.append(at("chunk2", 8 * CHUNK * EARLY + 4 * DC * P, [P, CHUNK], F32))
        late = [at(f"late{c}", LATE_AT + 4 * CHUNK * c, [P, CHUNK], F32) for c in range(4)] + chunk[0:2]
        x1 = [small(f"x1{u}", [P, D]) for u in range(2)]
        y_out += [at(f"y_out{u + 2}", AB + 6 * RB + 4 * D * (2 + u), [P, D], F32) for u in range(2)]
        row = [small(f"row{u}", [P, D]) for u in range(2)]
        zeros = at("zeros", o, [P, D], F32)
        slot_in_tile = small("slot_in_tile", [P, TILES * TOP, P], F16)
        ident = small("ident", [P, P])
        before = small("before", [P, P], BF16)
        ones = small("ones", [P, P], BF16)
        iota_p = small("iota_p", [P, P], F16)
        rb = small("rb", [P, E])
        rw = small("rw", [P, DC, E])
        iota_j = small("iota_j", [P, SLOT_TILES])
        earlier = small("earlier", [P, E, E])
        token_1 = small("token_1", [P, TILES])
        real = small("real", [P, TILES])
        dump = small("dump", [P, 1])
        half = small("half", [P, 2])
        half_dinv = small("half_dinv", [P, TILES])
        chosen = small("chosen", [P, TILES, TOP, E])
        count = small("count", [P, TILES, E], BF16)
        tile_rank = small("tile_rank", [P, TILES * TOP])
        logits_all = small("logits_all", [P, TILES, E])
        gates = small("gates", [P, TILES, E])
        G = GROUPS[0]
        probs = small("probs", [P, G, E])
        best = small("best", [P, G, E])
        best_at = small("best_at", [P, G, E], U32)
        ranks = small("ranks", [P, G * TOP, E])
        first_of = small("first_of", [P, G])
        inv_sum = small("inv_sum", [P, G])
        rank = small("rank", [P, G * TOP])
        in_tile = small("in_tile", [P, G * TOP])
        stats = small("stats", [P, 6])
        minus_mean = [small(f"minus_mean{u}", [P, 1]) for u in range(2)]
        mv = small("mv", [P, 2])
        pow_in = [small(f"pow_in{u}", [P, 2]) for u in range(2)]
        pow_out = [small(f"pow_out{u}", [P, 2]) for u in range(2)]

        bank = [ctx.enter_context(nc.psum_tensor(f"bank{b}", [P, 512], F32)) for b in range(8)]
        z_bank = [bank[i] if i < STREAM else bank[i - STREAM] for i in range(TILES)]
        x1_bank = [bank[4], bank[5]]
        turn_bank = bank[6]
        logits = bank[7][:, 0:E]
        route_bank = [bank[3], bank[5]]
        xt_bank, h_bank, ht_bank, y_bank = bank[0:2], bank[2], bank[3], bank[4]

        rows_dram = nc.dram_tensor("rows_dram", [NP, ROW], F32, kind="Internal").ap()

        zeros_ready = sem("zeros_ready")
        consts = sem("consts")
        small_in = sem("small_in")
        x_rows_loaded = sems("x_rows_loaded")
        adj_in = sems("adj_in")
        power_ready = sem("power_ready")
        scale_ready = sem("scale_ready")
        sum_ready = sem("sum_ready")
        half_ready = sem("half_ready")
        mean_ready = sem("mean_ready")
        centred = sem("centred")
        stream_hi_ready = sem("stream_hi_ready")
        keep_hi_ready = sem("keep_hi_ready")
        y_hi_ready = sem("y_hi_ready")
        stream_lo_ready = sem("stream_lo_ready")
        stream_lo2_ready = sem("stream_lo2_ready")
        keep_lo_ready = sem("keep_lo_ready")
        y_lo_ready = sem("y_lo_ready")
        stream_used = sem("stream_used")
        z_done = sem("z_done")
        z_hi_ready = sem("z_hi_ready")
        z_lo_ready = sem("z_lo_ready")
        col_in = sems("col_in")
        x_in = sems("x_in")
        col_hi_ready = sem("col_hi_ready")
        col_lo_ready = sem("col_lo_ready")
        col_lo2_ready = sem("col_lo2_ready")
        col_used = sem("col_used")
        x1_ready = sem("x1_ready")
        x1_stored = sems("x1_stored")
        var_ready = sem("var_ready")
        rstd_ready = sem("rstd_ready")
        xn_ready = sem("xn_ready")
        turned = sem("turned")
        xn_t_ready = sem("xn_t_ready")
        logits_done = sem("logits_done")
        logits_ready = sem("logits_ready")
        shifted = sem("shifted")
        exp_ready = sem("exp_ready")
        gates_ready = sem("gates_ready")
        gates_stored = sem("gates_stored")
        row_stored = sems("row_stored")
        count_ready = sem("count_ready")
        rank_done = sem("rank_done")
        chunk_in = sems("chunk_in", PER_TILE)
        late_in = sems("late_in", CHUNKS - EARLY)
        chunk_hi_ready = sem("chunk_hi_ready")
        chunk_lo_ready = sem("chunk_lo_ready")
        bias_in = sems("bias_in")
        zeros_stored = sem("zeros_stored")
        place_ready = sem("place_ready")
        token_done = sem("token_done")
        index_ready = sem("index_ready")
        from_set = sem("from_set")
        to_set = sem("to_set")
        gathered = sems("gathered")
        xt_done = sem("xt_done")
        xt_hi_ready = sem("xt_hi_ready")
        xt_lo_ready = sem("xt_lo_ready")
        gate_ready = sem("gate_ready")
        h_done = sem("h_done")
        h_sum_ready = sem("h_sum_ready")
        h_ready = sem("h_ready")
        ht_done = sem("ht_done")
        ht_hi_ready = sem("ht_hi_ready")
        ht_lo_ready = sem("ht_lo_ready")
        y_done = sem("y_done")
        y_sum_ready = sem("y_sum_ready")
        y_out_ready = sem("y_out_ready")
        added = sems("added")
        dve_step = sem("dve_step")
        dve_passed = sem("dve_passed")
        pool_passed = sem("pool_passed")
        pool_step = sem("pool_step")

        def over(eng, count, peeled, looped, step, turns_of=2, start=0):
            def straight(n):
                step(n, n % turns_of, n // 2 + 1)

            for n in range(start, peeled):
                straight(n)
            with eng.Fori(0, looped // turns_of) as turn:
                for v in range(turns_of):
                    n = peeled + v
                    step(turn * turns_of + n, n % turns_of, turn * (turns_of // 2) + n // 2 + 1)
            for n in range(peeled + looped, count):
                straight(n)

        def over_tiles(eng, step):
            over(eng, TILES, 3, TILES - 5, step)


        def works(n, lag):
            return not isinstance(n, int) or 0 <= n - lag < SLOT_TILES

        def expert_at(eng, n):
            return nc.values_load(expert_of[0:1, ds(n, 1)], engines=(eng.engine,), min_val=0, max_val=E - 1,
                                  skip_runtime_bounds_check_because="it is written as a minimum with E - 1 "
                                                                    "of a count")

        def weights_at(part, e, first_chunk, chunks, at, columns):
            all_experts = w_parts[:, first_chunk:first_chunk + E * chunks, :, :]
            at = at // CHUNK * 2 * CHUNK + part * CHUNK + at % CHUNK
            return all_experts.rearrange("p (e n) h c -> p e (n h c)", e=E)[:, ds(e, 1), at:at + columns
                                                                            ].rearrange("p e c -> p (e c)")

        def w1(part, e, c):
            return weights_at(part, e, 0, W2_CHUNK // E, c * FE, FE)

        def w2(part, e, c):
            return weights_at(part, e, W2_CHUNK, (CHUNKS - W2_CHUNK) // E, c * D, D)

        def chunk_at(part, c):
            return w_parts[:, ds(c, 1), part, :].rearrange("p k c -> p (k c)")

        def chunks_of(i):
            return range(PER_TILE if not isinstance(i, int) else max(0, min(PER_TILE, EARLY - PER_TILE * i)))

        def late_chunk(c):
            return EARLY + (c + 1) % (CHUNKS - EARLY)

        def ranks_of(g):
            return route_bank[g][:, 0:GROUPS[g] * E]

        def totals_of(g):
            return route_bank[g][:, 128:128 + E]

        def tokens_of(g):
            return route_bank[g][:, 256:256 + (SLOT_TILES - A_TILES if g else A_TILES)]

        block = ctx.enter_context(nc.Block())

        @block.sync
        def _(sp):
            def load_rows(k, u, use):
                if not isinstance(k, int) or k >= 2:
                    sp.wait_ge(sum_ready, k - 1)
                    sp.wait_ge(mean_ready, k - 1)
                sp.dma_start(x_rows_in[:, ds(k, 1), :].rearrange("p k c -> p (k c)"),
                             x_rows[ds(k * P, P), :]).then_inc(x_rows_loaded[u], 16)
                sp.dma_start(a_row[u][:, :], adj_rows[ds(k * P, P), :]).then_inc(adj_in[u], 16)
                sp.dma_start(at_row[u][:, :], adjt_rows[ds(k * P, P), :]).then_inc(adj_in[u], 16)

            over_tiles(sp, load_rows)

            def load_col(i, u):
                sp.dma_start(col[u][:, :], adjt_cols[ds(i * P, P), :]).then_inc(col_in[u], 16)

            def load_x(i, u):
                sp.dma_start(x1[u][:, :], x_rows[ds(i * P, P), :]).then_inc(x_in[u], 16)

            def load_chunk(c, j):
                if not isinstance(c, int) or c >= PER_TILE:
                    sp.wait_ge(chunk_lo_ready, c - (PER_TILE - 1))
                sp.dma_start(chunk[j][:, :], weights[ds(c * P, P), :]).then_inc(chunk_in[j], 16)

            sp.dma_start(rw[:, :, :], router_w).then_inc(small_in, 16)
            sp.dma_start(rb[:, :], router_b.broadcast_to([P, E])).then_inc(small_in, 16)
            sp.wait_ge(sum_ready, TILES)
            for i in range(2):
                load_x(i, i)
                load_col(i, i)
            sp.wait_ge(zeros_ready, 1)
            sp.dma_start(out[N:OUT_ROWS, :], zeros[:, :]).then_inc(zeros_stored, 16)

            def store_gates(g):
                a, b = sum(GROUPS[:g]), sum(GROUPS[:g + 1])
                sp.wait_ge(gates_ready, g + 1)
                sp.dma_start(rows_dram[a * P:b * P, D:ROW].rearrange("(i p) e -> p i e", p=P),
                             gates[:, a:b, :]).then_inc(gates_stored, 16)

            def store_tile(i, u, rows=P):
                sp.wait_ge(x1_ready, i + 1)
                sp.dma_start(out[ds(i * P, rows), :], x1[u][0:rows, :]).then_inc(x1_stored[u], 16)
                sp.wait_ge(xn_ready, i + 1)
                sp.dma_start(rows_dram[ds(i * P, P), 0:D], row[u][:, :]).then_inc(row_stored[u], 16)

            def serve_tile(i, u, use):
                sp.wait_ge(col_lo_ready, i + 1)
                sp.wait_ge(col_lo2_ready, i + 1)
                load_col(i + 2, u)
                for j in chunks_of(i):
                    load_chunk(i * PER_TILE + j, j)
                store_tile(i, u)
                sp.wait_ge(x1_stored[u], 16 * use)
                load_x(i + 2, u)

            over(sp, TILES - 2, 3, TILES - 7, serve_tile)
            store_gates(0)
            store_tile(TILES - 2, (TILES - 2) % 2)
            sp.wait_ge(col_used, TILES)
            for c in range(CHUNKS - EARLY):
                sp.dma_start(late[c][:, :], weights[late_chunk(c) * P:(late_chunk(c) + 1) * P, :]
                             ).then_inc(late_in[c], 16)
            store_tile(TILES - 1, (TILES - 1) % 2, LAST)
            sp.wait_ge(xt_done, 1)
            sp.dma_start(b1_all[:, :], b1.broadcast_to([P, E * FE])).then_inc(bias_in[0], 16)
            for h in range(2):
                sp.wait_ge(xt_done, 2 + h)
                if h:
                    store_gates(1)
                half_e = slice(h * E * D // 2, (h + 1) * E * D // 2)
                sp.dma_start(b2_all[:, half_e], b2[:, half_e].broadcast_to([P, E * D // 2])
                             ).then_inc(bias_in[1], 16)

        @block.gpsimd
        def _(pool):
            pool.memset(zeros[:, :], 0.0).then_inc(zeros_ready, 1)
            pool.memset(half[:, :], -0.5).then_inc(pool_step, 1)
            pool.memset(ident[:, :], 0.0).then_inc(pool_step, 1)
            pool.memset(before[:, :], 1.0).then_inc(pool_step, 1)
            pool.memset(earlier[:, :, :], 1.0).then_inc(pool_step, 1)
            pool.memset(real[:, :], 1.0).then_inc(pool_step, 1)
            pool.memset(ones[:, :], 1.0).then_inc(pool_step, 1)
            pool.iota(iota_p[:, :], pattern=[[1, P]], base=0, channel_multiplier=0,
                      allow_small_or_imprecise_dtypes=True).then_inc(pool_step, 1)
            pool.iota(iota_j[:, :], pattern=[[1, SLOT_TILES]], base=0, channel_multiplier=0,
                      allow_small_or_imprecise_dtypes=True).then_inc(pool_step, 1)
            pool.iota(token_1[:, :], pattern=[[P, TILES]], base=1, channel_multiplier=1,
                      allow_small_or_imprecise_dtypes=True).then_inc(pool_step, 1)
            pool.iota(dump[:, :], pattern=[[0, 1]], base=N + 1, channel_multiplier=1,
                      allow_small_or_imprecise_dtypes=True).then_inc(pool_step, 1)
            pool.memset(plus_half[:, :], 0.5).then_inc(pool_step, 1)
            OWN = 11
            pool.wait_ge(pool_step, OWN)
            pool.affine_select(out=ident[:, :], in_=ident[:, :], compare_op=ALU.not_equal, fill=1.0,
                               base=0, pattern=[[-1, P]], channel_multiplier=1).then_inc(consts, 1)
            pool.affine_select(out=before[:, :], in_=before[:, :], compare_op=ALU.is_gt, fill=0.0,
                               base=0, pattern=[[1, P]], channel_multiplier=-1).then_inc(consts, 1)
            pool.affine_select(out=earlier[:, :, :], in_=earlier[:, :, :], compare_op=ALU.is_gt, fill=0.0,
                               base=0, pattern=[[1, E], [-1, E]], channel_multiplier=0).then_inc(consts, 1)
            pool.affine_select(out=token_1[:, :], in_=token_1[:, :], compare_op=ALU.is_ge, fill=0.0,
                               base=N - 1, pattern=[[-P, TILES]], channel_multiplier=-1).then_inc(consts, 1)
            pool.affine_select(out=real[:, :], in_=real[:, :], compare_op=ALU.is_ge, fill=0.0,
                               base=N - 1, pattern=[[-P, TILES]], channel_multiplier=-1).then_inc(consts, 1)

            def rows(k, u, use):
                before_tile = k * 2 + OWN
                pool.wait_ge(power_ready, k + 1)
                if not isinstance(k, int) or k >= 1:
                    pool.wait_ge(scale_ready, k)
                    pool.wait_ge(half_ready, k)
                pool.tensor_tensor(powers[:, :], power_in[u][:, :], half[:, :], ALU.pow).then_inc(pool_step, 1)
                pool.wait_ge(pool_step, before_tile + 1)
                pool.tensor_tensor(dinv[:, :], powers[:, 0:1], positive[u][:, :], ALU.mult).then_inc(pool_step, 1)
                pool.wait_ge(pool_step, before_tile + 2)
                pool.tensor_tensor(y_scale[u][:, :], dinv[:, :], powers[:, 1:2], ALU.mult
                                   ).then_inc(scale_ready, 1)
                pool.tensor_tensor(half_dinv[:, ds(k, 1)], dinv[:, :], plus_half[:, :], ALU.mult
                                   ).then_inc(half_ready, 1)
                pool.wait_ge(stream_hi_ready, k + 1)
                pool.tensor_tensor(stream_lo[u][:, LOW:SC], sum_row[u][:, LOW:SC],
                                   stream_hi[u][:, LOW:SC].bitcast(F32), ALU.subtract).then_inc(stream_lo2_ready, 1)
                pool.wait_ge(keep_hi_ready, k + 1)
                pool.tensor_tensor(keep_lo[:, ds(k, 1), :].rearrange("p k c -> p (k c)"),
                                   sum_row[u][:, SC:NP],
                                   keep_hi[:, ds(k, 1), :].rearrange("p k c -> p (k c)").bitcast(F32),
                                   ALU.subtract).then_inc(keep_lo_ready, 1)

            over_tiles(pool, rows)

            def split_col(i, u):
                pool.wait_ge(col_hi_ready, i + 1)
                pool.tensor_tensor(col_lo[u][:, NP // 2:], col[u][:, NP // 2:],
                                   col_hi[u][:, NP // 2:].bitcast(F32), ALU.subtract).then_inc(col_lo_ready, 1)

            def split_chunk(c, u):
                pool.wait_ge(chunk_hi_ready, c + 1)
                pool.tensor_tensor(chunk_at(1, c), chunk[u][:, :], chunk_at(0, c).bitcast(F32),
                                   ALU.subtract).then_inc(chunk_lo_ready, 1)

            def power(i, u):
                pool.wait_ge(var_ready, i + 1)
                pool.tensor_tensor(pow_out[u][:, 0:1], pow_in[u][:, 0:1], half[:, 0:1],
                                   ALU.pow).then_inc(rstd_ready, 1)

            pool.wait_ge(stream_lo_ready, TILES)
            pool.wait_ge(keep_lo_ready, TILES)
            pool.wait_ge(stream_lo2_ready, TILES)
            split_col(0, 0)
            split_col(1, 1)
            pool.wait_ge(z_done, TILES)

            def serve_tile(i, u, use):
                power(i, u)
                split_col(i + 2, u)
                for j in chunks_of(i):
                    split_chunk(i * PER_TILE + j, j)

            over(pool, TILES - 2, 3, TILES - 7, serve_tile)
            power(TILES - 2, (TILES - 2) % 2)

            def fetch(n, q):
                u = q % 2
                if isinstance(n, int) and n == A_TILES:
                    pool.wait_ge(index_ready, 4)
                    pool.wait_ge(gates_stored, 32)
                    for v in range(2):
                        pool.wait_ge(row_stored[v], 16 * ((TILES - v + 1) // 2))
                if not isinstance(n, int) or n >= 2:
                    pool.wait_ge(xt_done, n - 1)
                    pool.wait_ge(gate_ready, n - 1)
                pool.tensor_copy(from_now[u][:, :], from_row[:, ds(n, 1)]).then_inc(from_set, 1)
                pool.wait_ge(from_set, n + 1)
                pool.sem_inc(pool_passed, 1)
                first_ones = isinstance(n, int) and n < A_TILES
                pool.indirect_dma_start(xg[u][:, :], None,
                                        rows_dram[0:GROUPS[0] * P, :] if first_ones else rows_dram,
                                        bass.IndirectOffsetOnAxis(ap=from_now[u][:, :], axis=0)
                                        ).then_inc(gathered[u], 16)

            def add(n, q, use):
                u, w = q % 2, (q - LAG) % 2
                before = use - 1 - (LAG - u) // 2
                if isinstance(n, int) and n == LAG:
                    pool.wait_ge(zeros_stored, 16)
                    for v in range(2):
                        pool.wait_ge(x1_stored[v], 16 * ((TILES - v + 1) // 2))
                pool.tensor_copy(to_now[w][:, :], to_row[:, ds(n - LAG, 1)]).then_inc(to_set, 1)
                pool.wait_ge(y_out_ready, n - (LAG - 1))
                pool.wait_ge(to_set, n - (LAG - 1))
                if not isinstance(n, int) or n >= LAG + 1:
                    pool.wait_ge(added[1 - w], 16 * before)
                pool.sem_inc(pool_passed, 1)
                pool.indirect_dma_start(out,
                                        bass.IndirectOffsetOnAxis(ap=to_now[w][:, :], axis=0),
                                        y_out[(q - LAG) % 4][:, :], None, compute_op=ALU.add
                                        ).then_inc(added[w], 16)

            def slots(n, q, use):
                early = isinstance(n, int) and n < PEELED
                if early and works(n, LAG):
                    add(n, q, use)
                if works(n, 0):
                    fetch(n, q)
                if not early and works(n, LAG):
                    add(n, q, use)

            pool.wait_ge(index_ready, 2)
            pool.wait_ge(gates_stored, 16)
            for u in range(2):
                pool.wait_ge(row_stored[u], 16 * ((TILES - 1 - u + 1) // 2))
            slots(0, 0, 1)
            power(TILES - 1, (TILES - 1) % 2)
            slots(1, 1, 1)
            for c in range(CHUNKS - EARLY):
                if c in (2, 4):
                    slots(c // 2 + 1, c // 2 + 1, 2)
                pool.wait_ge(chunk_hi_ready, EARLY + c + 1)
                pool.tensor_tensor(chunk_at(1, late_chunk(c)), late[c][:, :], chunk_at(0, late_chunk(c)).bitcast(F32),
                                   ALU.subtract).then_inc(chunk_lo_ready, 1)
            over(pool, SLOT_TILES + LAG, PEELED, (SLOT_TILES - PEELED) // 4 * 4, slots, 4, start=4)
            for u in range(2):
                pool.wait_ge(added[u], 16 * ((SLOT_TILES - u + 1) // 2))

        @block.scalar
        def _(act):
            def rows(k, u, use):
                act.wait_ge(mean_ready, k + 1)
                if not isinstance(k, int) or k >= 2:
                    act.wait_ge(y_lo_ready, k - 1)
                act.activation(x_less_mean[u][:, :], x_rows_in[:, ds(k, 1), :].rearrange("p k c -> p (k c)"),
                               ACT.Identity, bias=minus_mean[u][:, :]).then_inc(centred, 1)
                act.wait_ge(sum_ready, k + 1)
                if not isinstance(k, int) or k >= 2:
                    act.wait_ge(stream_used, k - 1)
                act.activation(stream_hi[u][:, :], sum_row[u][:, 0:SC], ACT.Copy).then_inc(stream_hi_ready, 1)
                act.activation(keep_hi[:, ds(k, 1), :].rearrange("p k c -> p (k c)"), sum_row[u][:, SC:NP],
                               ACT.Copy).then_inc(keep_hi_ready, 1)
                act.wait_ge(scale_ready, k + 1)
                act.wait_ge(centred, k + 1)
                act.activation(y_hi[:, ds(k, 1), :].rearrange("p k c -> p (k c)"), x_less_mean[u][:, :],
                               ACT.Copy, scale=y_scale[u][:, :]).then_inc(y_hi_ready, 1)

            over_tiles(act, rows)

            def split_col(i, u, use):
                act.wait_ge(col_in[u], 16 * use)
                if not isinstance(i, int) or i >= 2:
                    act.wait_ge(col_used, i - 1)
                act.activation(col_hi[u][:, :], col[u][:, :], ACT.Copy).then_inc(col_hi_ready, 1)

            def split_chunk(c, u, use):
                act.wait_ge(chunk_in[u], 16 * use)
                act.activation(chunk_at(0, c), chunk[u][:, :], ACT.Copy).then_inc(chunk_hi_ready, 1)

            act.wait_ge(sum_ready, TILES)
            split_col(0, 0, 1)
            split_col(1, 1, 1)
            act.wait_ge(half_ready, TILES)
            for i in range(TILES):
                act.wait_ge(z_done, i + 1)
                act.activation(z_hi[:, i, :], z_bank[i][:, :], ACT.Copy,
                               scale=half_dinv[:, i:i + 1]).then_inc(z_hi_ready, 1)

            def take_turned(i):
                act.wait_ge(turned, i + 1)
                if not isinstance(i, int) or i >= 1:
                    act.wait_ge(logits_done, i)
                act.activation(xn_t[:, :, :].rearrange("p c q -> p (c q)"), turn_bank[:, :],
                               ACT.Copy).then_inc(xn_t_ready, 1)

            def serve_tile(i, u, use):
                split_col(i + 2, u, use + 1)
                take_turned(i)
                for j in chunks_of(i):
                    split_chunk(i * PER_TILE + j, j, i + 1)

            def exponentials(g):
                act.wait_ge(shifted, g + 1)
                act.activation(probs[:, 0:GROUPS[g], :], probs[:, 0:GROUPS[g], :], ACT.Exp).then_inc(exp_ready, 1)

            def late_high(c):
                act.wait_ge(late_in[c], 16)
                act.activation(chunk_at(0, late_chunk(c)), late[c][:, :], ACT.Copy).then_inc(chunk_hi_ready, 1)

            over(act, TILES - 3, 3, TILES - 7, serve_tile)
            serve_tile(TILES - 3, 0, (TILES - 3) // 2 + 1)
            exponentials(0)
            take_turned(TILES - 2)
            for c in range(2):
                late_high(c)
            take_turned(TILES - 1)
            for c in range(2, CHUNKS - EARLY - 1):
                late_high(c)

            def slots(n, q, use):
                u, v = q % 2, 1 - q % 2
                if works(n, 0):
                    act.wait_ge(xt_done, n + 1)
                    if not isinstance(n, int) or n >= 2:
                        act.wait_ge(h_done, n - 1)
                    act.activation(xt_hi[u][:, :], xt_bank[u][:, :], ACT.Copy).then_inc(xt_hi_ready, 1)
                if works(n, 4):
                    act.wait_ge(y_sum_ready, n - 3)
                    if not isinstance(n, int) or n >= 8:
                        act.wait_ge(added[u], 16 * (use - 4))
                    act.activation(y_out[q][:, :], y_sum[u][:, :], ACT.Copy,
                                   scale=slot_gate[:, ds(n - 4, 1)]).then_inc(y_out_ready, 1)
                if works(n, 2):
                    act.wait_ge(ht_done, n - 1)
                    if not isinstance(n, int) or n >= 4:
                        act.wait_ge(y_done, n - 3)
                    act.activation(ht_hi[u][:, :], ht_bank[:, 0:FE], ACT.Copy).then_inc(ht_hi_ready, 1)
                if works(n, 1):
                    act.wait_ge(h_sum_ready, n)
                    if not isinstance(n, int) or n >= 3:
                        act.wait_ge(ht_done, n - 2)
                    act.activation(h_act[v][:, :], h_sum[v][:, :], ACT.Gelu).then_inc(h_ready, 1)

            slots(0, 0, 1)
            act.wait_ge(logits_done, TILES)
            late_high(CHUNKS - EARLY - 1)
            exponentials(1)
            for u in range(2):
                act.wait_ge(x1_stored[u], 16 * ((TILES - u + 1) // 2))
            over(act, SLOT_TILES + 4, PEELED, (SLOT_TILES - PEELED) // 4 * 4, slots, 4, start=1)

        @block.tensor
        def _(pe):
            def product(ps, hi, lo, rhs_hi, rhs_lo, start, stop):
                pe.matmul(ps, lo, rhs_hi, start=start, stop=False, skip_group_check=True)
                pe.matmul(ps, hi, rhs_lo, start=False, stop=False, skip_group_check=True)
                return pe.matmul(ps, hi, rhs_hi, start=False, stop=stop, skip_group_check=True)

            def y_at(part, k):
                return part[:, ds(k, 1), :].rearrange("p k c -> p (k c)")

            def rows(k, u, use):
                pe.wait_ge(y_lo_ready, k + 1)
                pe.wait_ge(stream_lo_ready, k + 1)
                pe.wait_ge(stream_lo2_ready, k + 1)
                for i in range(STREAM):
                    last = product(bank[i][:, :], stream_hi[u][:, i * P:(i + 1) * P],
                                   stream_lo[u][:, i * P:(i + 1) * P], y_at(y_hi, k), y_at(y_lo, k),
                                   isinstance(k, int) and k == 0, True)
                    if isinstance(k, int) and k == TILES - 1:
                        last.then_inc(z_done, 1)
                if not isinstance(k, int) or k < TILES - 1:
                    last.then_inc(stream_used, 1)

            over_tiles(pe, rows)
            pe.wait_ge(keep_lo_ready, TILES)
            for i in range(KEEP):
                pe.wait_ge(z_lo_ready, i + 1)
                for k in range(TILES):
                    last = product(z_bank[STREAM + i][:, :], keep_hi[:, k, i * P:(i + 1) * P],
                                   keep_lo[:, k, i * P:(i + 1) * P], y_hi[:, k, :], y_lo[:, k, :],
                                   k == 0, k == TILES - 1)
                last.then_inc(z_done, 1)

            def turn(i, u):
                pe.wait_ge(xn_ready, i + 1)
                if not isinstance(i, int) or i >= 1:
                    pe.wait_ge(xn_t_ready, i)
                for c in range(DC):
                    last = pe.transpose(turn_bank[:, c * P:(c + 1) * P], row[u][:, c * P:(c + 1) * P], ident[:, :])
                last.then_inc(turned, 1)

            def route(i):
                pe.wait_ge(xn_t_ready, i + 1)
                if not isinstance(i, int) or i >= 1:
                    pe.wait_ge(logits_ready, i)
                for c in range(DC):
                    last = pe.matmul(logits, xn_t[:, c, :], rw[:, c, :], start=c == 0, stop=c == DC - 1)
                last.then_inc(logits_done, 1)

            def rank_group(g):
                a, b = sum(GROUPS[:g]), sum(GROUPS[:g + 1])
                rank_ps, total_ps = ranks_of(g), totals_of(g)
                pe.wait_ge(count_ready, g + 1)
                pe.matmul(rank_ps[:, 0:(b - a) * E], before[:, :],
                          count[:, a:b, :].rearrange("p i e -> p (i e)"), start=True, stop=False)
                for i in range(b - 1):
                    at = max(i + 1, a)
                    pe.matmul(rank_ps[:, (at - a) * E:(b - a) * E], ones[:, :],
                              count[:, i:i + 1, :].broadcast_to([P, b - at, E]),
                              start=False, stop=i == b - 2)
                for i in range(b):
                    last = pe.matmul(total_ps, ones[:, :], count[:, i, :], start=i == 0, stop=i == b - 1)
                last.then_inc(rank_done, 1)

            def token_group(g):
                pe.wait_ge(place_ready, g + 1)
                m = sum(GROUPS[:g + 1]) * TOP
                for i in range(m):
                    last = pe.matmul(tokens_of(g), slot_in_tile[:, i, :], slot_token[g][:, i, :],
                                     start=i == 0, stop=i == m - 1)
                last.then_inc(token_done, 1)

            def columns(i, u, use):
                pe.wait_ge(col_lo_ready, i + 1)
                pe.wait_ge(col_lo2_ready, i + 1)
                if not isinstance(i, int) or i >= 2:
                    pe.wait_ge(x1_ready, i - 1)
                for k in range(TILES):
                    if isinstance(i, int) and i == 0:
                        pe.wait_ge(z_lo_ready, max(k + 1, 5))
                    last = product(x1_bank[u][:, :], col_hi[u][:, k * P:(k + 1) * P],
                                   col_lo[u][:, k * P:(k + 1) * P], z_hi[:, k, :], z_lo[:, k, :],
                                   k == 0, k == TILES - 1)
                    if k == TILES - 1:
                        last.then_inc(col_used, 1)
                    if not isinstance(i, int) or i >= 1:
                        late_turn = isinstance(i, int) and i == TILES - 1
                        if k == (8 if late_turn else 4):
                            turn(i - 1, 1 - u)
                        if k == (10 if late_turn else 7):
                            route(i - 1)
                        if isinstance(i, int) and (i, k) == RANK_AT:
                            rank_group(0)

            pe.wait_ge(small_in, 32)
            pe.wait_ge(consts, 5)
            over(pe, TILES, 3, TILES - 5, columns)
            def slots(n, u, use):
                v = 1 - u
                if works(n, 0):
                    pe.wait_ge(gathered[u], 16 * use)
                    if not isinstance(n, int) or n >= 2:
                        pe.wait_ge(xt_lo_ready, n - 1)
                    for c in range(DC):
                        last = pe.transpose(xt_bank[u][:, c * P:(c + 1) * P], xg[u][:, c * P:(c + 1) * P],
                                            ident[:, :])
                    last.then_inc(xt_done, 1)
                if isinstance(n, int) and n == A_TILES + 1:
                    pe.wait_ge(index_ready, 4)
                if works(n, 1):
                    e = expert_at(pe, n - 1)
                    pe.wait_ge(xt_lo_ready, n)
                    if not isinstance(n, int) or n >= 2:
                        pe.wait_ge(h_sum_ready, n - 1)
                    for c in range(DC):
                        last = product(h_bank[:, 0:FE], xt_hi[v][:, c * P:(c + 1) * P],
                                       xt_lo[v][:, c * P:(c + 1) * P], w1(0, e, c), w1(1, e, c),
                                       c == 0, c == DC - 1)
                    last.then_inc(h_done, 1)
                if works(n, 3):
                    e_y = expert_at(pe, n - 3)
                if works(n, 2):
                    pe.wait_ge(h_ready, n - 1)
                    if not isinstance(n, int) or n >= 3:
                        pe.wait_ge(ht_lo_ready, n - 2)
                    for c in range(FC):
                        last = pe.transpose(ht_bank[:, c * P:(c + 1) * P], h_act[u][:, c * P:(c + 1) * P],
                                            ident[:, :])
                    last.then_inc(ht_done, 1)
                if works(n, 3):
                    pe.wait_ge(ht_lo_ready, n - 2)
                    if not isinstance(n, int) or n >= 4:
                        pe.wait_ge(y_sum_ready, n - 3)
                    else:
                        pe.wait_ge(chunk_lo_ready, CHUNKS)
                    for c in range(FC):
                        last = product(y_bank[:, :], ht_hi[v][:, c * P:(c + 1) * P],
                                       ht_lo[v][:, c * P:(c + 1) * P], w2(0, e_y, c), w2(1, e_y, c),
                                       c == 0, c == FC - 1)
                    last.then_inc(y_done, 1)

            token_group(0)
            turn(TILES - 1, 0)
            pe.wait_ge(index_ready, 2)
            slots(0, 0, 1)
            route(TILES - 1)
            slots(1, 1, 1)
            rank_group(1)
            slots(2, 0, 2)
            slots(3, 1, 2)
            slots(4, 0, 3)
            token_group(1)
            over(pe, SLOT_TILES + 3, PEELED, (SLOT_TILES - PEELED) // 2 * 2, slots, start=5)

        @block.vector
        def _(dve):
            class Steps:
                base = 0
                n = 0

                def then(self, ins, apart=False):
                    self.n += 1
                    ins.then_inc(dve_step, 1)
                    dve.wait_ge(dve_step, self.base + self.n)
                    if apart:
                        dve.sem_inc(dve_passed, 1)

            own = Steps()

            def counted(per_tile, step, count, peeled, looped):
                start = own.base + own.n

                def one(k, u, use):
                    own.base, own.n = k * per_tile + start, 0
                    step(k, u, use)
                    assert own.n == per_tile, own.n

                over(dve, count, peeled, looped, one)
                own.base, own.n = start + count * per_tile, 0

            def rows(k, u, use):
                dve.wait_ge(x_rows_loaded[u], 16 * use)
                if not isinstance(k, int) or k >= 2:
                    dve.wait_ge(centred, k - 1)
                own.then(dve.bn_stats(stats[:, :], x_at(k)), apart=True)
                own.then(dve.bn_aggr(mv[:, :], stats[:, :]))
                dve.tensor_scalar(power_in[u][:, 1:2], mv[:, 1:2], EPS, None, ALU.add)
                dve.tensor_scalar(minus_mean[u][:, :], mv[:, 0:1], -1.0, None, ALU.mult).then_inc(mean_ready, 1)
                dve.wait_ge(adj_in[u], 32 * use)
                if not isinstance(k, int) or k >= 2:
                    dve.wait_ge(stream_lo_ready, k - 1)
                    dve.wait_ge(stream_lo2_ready, k - 1)
                    dve.wait_ge(keep_lo_ready, k - 1)
                    dve.sem_inc(dve_passed, 1)
                own.then(dve.tensor_tensor_reduce(sum_row[u][:, :], a_row[u][:, :], at_row[u][:, :], 1.0, 0.0,
                                                  ALU.add, ALU.add, row_sum[:, :]))
                dve.scalar_tensor_tensor(sum_row[u][:, ds(k * P, P)], ident[:, :], 2.0,
                                         sum_row[u][:, ds(k * P, P)], ALU.mult, ALU.add).then_inc(sum_ready, 1)
                own.then(dve.tensor_scalar(deg[:, :], row_sum[:, :], 0.5, 1.0, ALU.mult, ALU.add))
                dve.tensor_scalar(power_in[u][:, 0:1], deg[:, :], 1e-30, None, ALU.max)
                dve.tensor_scalar(positive[u][:, :], deg[:, :], 0.0, None, ALU.is_gt).then_inc(power_ready, 1)
                if isinstance(k, int) and k == 0:
                    low_part(0, 0)
                elif not isinstance(k, int) or k >= 2:
                    low_part(k - 1, 1 - u)

            def x_at(k):
                return x_rows_in[:, ds(k, 1), :].rearrange("p k c -> p (k c)")

            def low_part(k, u):
                dve.wait_ge(stream_hi_ready, k + 1)
                dve.tensor_tensor(stream_lo[u][:, 0:LOW], sum_row[u][:, 0:LOW], stream_hi[u][:, 0:LOW].bitcast(F32),
                                  ALU.subtract).then_inc(stream_lo_ready, 1)
                dve.wait_ge(y_hi_ready, k + 1)
                dve.scalar_tensor_tensor(y_lo[:, ds(k, 1), :].rearrange("p k c -> p (k c)"), x_less_mean[u][:, :],
                                         y_scale[u][:, :],
                                         y_hi[:, ds(k, 1), :].rearrange("p k c -> p (k c)").bitcast(F32),
                                         ALU.mult, ALU.subtract).then_inc(y_lo_ready, 1)

            dve.wait_ge(consts, 5)
            counted(4, rows, TILES, 3, TILES - 5)
            low_part(TILES - 1, 0)

            def split_col(i, u):
                dve.wait_ge(col_hi_ready, i + 1)
                dve.tensor_tensor(col_lo[u][:, 0:NP // 2], col[u][:, 0:NP // 2],
                                  col_hi[u][:, 0:NP // 2].bitcast(F32), ALU.subtract).then_inc(col_lo2_ready, 1)

            dve.wait_ge(stream_lo2_ready, TILES)
            dve.wait_ge(keep_lo_ready, TILES)
            dve.wait_ge(stream_lo_ready, TILES)
            split_col(0, 0)
            split_col(1, 1)
            for i in range(TILES):
                dve.wait_ge(z_hi_ready, i + 1)
                dve.scalar_tensor_tensor(z_lo[:, i, :], z_bank[i][:, :], half_dinv[:, i:i + 1],
                                         z_hi[:, i, :].bitcast(F32), ALU.mult, ALU.subtract).then_inc(z_lo_ready, 1)
            dve.wait_ge(small_in, 32)
            dve.wait_ge(zeros_stored, 16)

            def take_logits(i):
                dve.wait_ge(logits_done, i + 1)
                dve.tensor_tensor(logits_all[:, ds(i, 1), :].rearrange("p i e -> p (i e)"), logits, rb[:, :],
                                  ALU.add).then_inc(logits_ready, 1)

            def norm_tile(i, u, use):
                norm_begin(i, u, use)
                if not isinstance(i, int) or i >= 1:
                    take_logits(i - 1)
                norm_end(i, u, use)
                if not isinstance(i, int) or i <= TILES - 3:
                    split_col(i + 2, u)

            def norm_begin(i, u, use):
                dve.wait_ge(x_in[u], 16 * use)
                dve.wait_ge(col_used, i + 1)
                dve.tensor_tensor(x1[u][:, :], x1_bank[u][:, :], x1[u][:, :], ALU.add).then_inc(x1_ready, 1)
                dve.wait_ge(x1_ready, i + 1)
                own.then(dve.bn_stats(stats[:, :], x1[u][:, :]), apart=True)
                own.then(dve.bn_aggr(mv[:, :], stats[:, :]))
                dve.tensor_scalar(pow_in[u][:, 0:1], mv[:, 1:2], EPS, None, ALU.add).then_inc(var_ready, 1)

            def norm_end(i, u, use):
                if not isinstance(i, int) or i >= 2:
                    dve.wait_ge(row_stored[u], 16 * (use - 1))
                dve.wait_ge(rstd_ready, i + 1)
                dve.tensor_scalar(row[u][:, :], x1[u][:, :], mv[:, 0:1], pow_out[u][:, 0:1],
                                  ALU.subtract, ALU.mult).then_inc(xn_ready, 1)

            def first_half(g):
                a, b = sum(GROUPS[:g]), sum(GROUPS[:g + 1])
                n = b - a
                pr, peak, inv = probs[:, 0:n, :], first_of[:, 0:n], inv_sum[:, 0:n]
                dve.wait_ge(logits_ready, b)
                own.then(dve.tensor_reduce(peak, logits_all[:, a:b, :], AX_X, ALU.max))
                dve.tensor_tensor(pr, logits_all[:, a:b, :], peak[:, :, None].broadcast_to([P, n, E]),
                                  ALU.subtract).then_inc(shifted, 1)
                dve.wait_ge(exp_ready, g + 1)
                own.then(dve.tensor_reduce(inv, pr, AX_X, ALU.add))
                own.then(dve.reciprocal(inv, inv))
                own.then(dve.tensor_tensor(pr, pr, inv[:, :, None].broadcast_to([P, n, E]), ALU.mult))
                for i in range(n):
                    last = dve.max(best[:, i, :], probs[:, i, :])
                own.then(last)

            def second_half(g):
                a, b = sum(GROUPS[:g]), sum(GROUPS[:g + 1])
                n = b - a
                inv, both = inv_sum[:, 0:n], chosen[:, a:b, :, :]
                expert, gate = (t[:, 0:n * TOP].rearrange("p (i t) -> p i t", t=TOP) for t in (rank, in_tile))
                for i in range(n):
                    last = dve.max_index(best_at[:, i, :], best[:, i, :], probs[:, i, :])
                own.then(last)
                own.then(dve.tensor_copy(expert, best_at[:, 0:n, 0:TOP]))
                dve.tensor_tensor(both, iota_j[:, None, None, 0:E].broadcast_to([P, n, TOP, E]),
                                  expert[:, :, :, None].broadcast_to([P, n, TOP, E]), ALU.is_equal)
                own.then(dve.tensor_tensor(inv, best[:, 0:n, 0], best[:, 0:n, 1], ALU.add))
                own.then(dve.reciprocal(inv, inv))
                own.then(dve.tensor_tensor(gate, best[:, 0:n, 0:TOP],
                                           inv[:, :, None].broadcast_to([P, n, TOP]), ALU.mult))
                gated = ranks[:, 0:n * TOP, :].rearrange("p (i t) e -> p i t e", t=TOP)
                own.then(dve.tensor_tensor(gated, both, gate[:, :, :, None].broadcast_to([P, n, TOP, E]), ALU.mult))
                dve.tensor_tensor(gates[:, a:b, :], gated[:, :, 0, :], gated[:, :, 1, :], ALU.add
                                  ).then_inc(gates_ready, 1)
                if b == TILES:
                    own.then(dve.tensor_tensor(
                        both.rearrange("p i t e -> p i (t e)"), both.rearrange("p i t e -> p i (t e)"),
                        real[:, a:b, None].broadcast_to([P, n, TOP * E]), ALU.mult))
                dve.tensor_tensor(count[:, a:b, :], both[:, :, 0, :], both[:, :, 1, :], ALU.add
                                  ).then_inc(count_ready, 1)

            def place_group(g):
                a, b = sum(GROUPS[:g]), sum(GROUPS[:g + 1])
                n, m = b - a, (b - a) * TOP
                dve.wait_ge(rank_done, g + 1)
                own.then(dve.tensor_tensor(
                    ranks[:, 0:m, :].rearrange("p (i t) e -> p i t e", t=TOP), chosen[:, a:b, :, :],
                    ranks_of(g).rearrange("p (i e) -> p i e", e=E)[:, :, None, :].broadcast_to([P, n, TOP, E]),
                    ALU.mult))
                own.then(dve.tensor_reduce(rank[:, 0:m], ranks[:, 0:m, :], AX_X, ALU.add))
                rank_i = best_at[:, :, :].rearrange("p i e -> p (i e)")[:, 0:m]
                own.then(dve.tensor_copy(rank_i, rank[:, 0:m]))
                own.then(dve.tensor_scalar(rank_i, rank_i, P - 1, None, ALU.bitwise_and))
                own.then(dve.tensor_copy(in_tile[:, 0:m], rank_i))
                dve.tensor_tensor(tile_rank[:, a * TOP:b * TOP], rank[:, 0:m], in_tile[:, 0:m], ALU.subtract)
                for c in range(m):
                    dve.tensor_scalar(slot_in_tile[:, a * TOP + c, :], iota_p[:, :], in_tile[:, c:c + 1],
                                      None, ALU.is_equal)

            def map_group(g):
                m = sum(GROUPS[:g + 1]) * TOP
                j0, j1 = (A_TILES, SLOT_TILES) if g else (0, A_TILES)
                own.then(dve.tensor_scalar(total_i[:, :], totals_of(g), float((P - 1) * g), None, ALU.add))
                own.then(dve.tensor_scalar(size_i[:, :], total_i[:, :], P.bit_length() - 1, None,
                                           ALU.arith_shift_right))
                own.then(dve.tensor_copy(size[:, :], size_i[:, :]))
                if g:
                    own.then(dve.tensor_tensor(size[:, :], size[:, :], taken[:, :], ALU.subtract))
                own.then(dve.tensor_tensor(size_before[:, :, :], earlier[:, :, :],
                                           size[:, None, :].broadcast_to([P, E, E]), ALU.mult))
                own.then(dve.tensor_reduce(first[:, :], size_before[:, :, :], AX_X, ALU.add))
                dve.tensor_tensor(end[:, :], first[:, :], size[:, :], ALU.add)
                if g:
                    own.then(dve.tensor_tensor(shift[:, :], first[:, :], taken[:, :], ALU.subtract))
                else:
                    own.then(dve.tensor_scalar(taken[:, :], first[:, :], -1.0, float(A_TILES), ALU.mult, ALU.add))
                    own.then(dve.scalar_tensor_tensor(taken[:, :], taken[:, :], 0.0, size[:, :], ALU.max, ALU.min))
                    own.then(dve.tensor_copy(shift[:, :], first[:, :]))
                def of_choice(result, of_expert):
                    own.then(dve.tensor_tensor(start_sel[:, 0:m, :],
                                               chosen[:, 0:m // TOP, :, :].rearrange("p i t e -> p (i t) e"),
                                               of_expert[:, None, :].broadcast_to([P, m, E]), ALU.mult))
                    own.then(dve.tensor_reduce(result[:, 0:m], start_sel[:, 0:m, :], AX_X, ALU.add))

                of_choice(tile_of, shift)
                of_choice(limit, taken)
                dve.scalar_tensor_tensor(tile_of[:, 0:m], tile_rank[:, 0:m], 1.0 / P, tile_of[:, 0:m],
                                         ALU.mult, ALU.add)
                own.then(dve.scalar_tensor_tensor(valid[:, 0:m], tile_rank[:, 0:m], 1.0 / P, limit[:, 0:m],
                                                  ALU.mult, ALU.is_ge if g else ALU.is_lt))
                own.then(dve.tensor_tensor(
                    valid[:, 0:m].rearrange("p (i t) -> p i t", t=TOP),
                    valid[:, 0:m].rearrange("p (i t) -> p i t", t=TOP),
                    token_1[:, 0:m // TOP, None].broadcast_to([P, m // TOP, TOP]), ALU.mult))
                own.then(dve.tensor_tensor(slot_token[g][:, :, :],
                                           iota_j[:, None, 0:j1 - j0].broadcast_to([P, m, j1 - j0]),
                                           tile_of[:, 0:m, None].broadcast_to([P, m, j1 - j0]), ALU.is_equal))
                dve.tensor_tensor(slot_token[g][:, :, :], slot_token[g][:, :, :],
                                  valid[:, 0:m, None].broadcast_to([P, m, j1 - j0]), ALU.mult
                                  ).then_inc(place_ready, 1)
                own.then(dve.tensor_tensor(over_j[:, 0:j1 - j0, :], end[0:1, None, :].broadcast_to([1, j1 - j0, E]),
                                           iota_j[0:1, 0:j1 - j0, None].broadcast_to([1, j1 - j0, E]), ALU.is_le))
                own.then(dve.tensor_reduce(expert_f[:, j0:j1], over_j[:, 0:j1 - j0, :], AX_X, ALU.add))
                dve.tensor_scalar(expert_of[:, j0:j1], expert_f[:, j0:j1], float(E - 1), None, ALU.min
                                  ).then_inc(index_ready, 1)

            def index_group(g):
                j = slice(A_TILES, SLOT_TILES) if g else slice(0, A_TILES)
                dve.wait_ge(token_done, g + 1)
                dve.tensor_scalar(token_0[:, j], tokens_of(g), -1.0, None, ALU.add)
                own.then(dve.tensor_scalar(empty[:, j], tokens_of(g), 0.0, None, ALU.is_equal))
                dve.tensor_scalar(from_row[:, j], token_0[:, j], 0.0, None, ALU.max)
                dve.scalar_tensor_tensor(to_row[:, j], empty[:, j], dump[:, :], token_0[:, j],
                                         ALU.mult, ALU.add).then_inc(index_ready, 1)

            counted(2, norm_tile, TILES - 3, 3, TILES - 7)
            norm_tile(TILES - 3, 0, (TILES - 3) // 2 + 1)
            first_half(0)
            second_half(0)
            norm_begin(TILES - 2, 1, TILES // 2)
            take_logits(TILES - 3)
            place_group(0)
            norm_end(TILES - 2, 1, TILES // 2)
            map_group(0)
            index_group(0)
            norm_begin(TILES - 1, 0, TILES // 2 + 1)
            take_logits(TILES - 2)
            norm_end(TILES - 1, 0, TILES // 2 + 1)
            dve.wait_ge(index_ready, 2)
            def slots(n, u, use):
                v = 1 - u
                if works(n, 4):
                    e = expert_at(dve, n - 4)
                    dve.wait_ge(y_done, n - 3)
                    if not isinstance(n, int) or n >= 6:
                        dve.wait_ge(y_out_ready, n - 5)
                    dve.tensor_tensor(y_sum[u][:, :], y_bank[:, :], b2_all[:, ds(e * D, D)],
                                      ALU.add).then_inc(y_sum_ready, 1)
                if works(n, 0):
                    e = expert_at(dve, n)
                    dve.wait_ge(xt_hi_ready, n + 1)
                    dve.tensor_tensor(xt_lo[u][:, :], xt_bank[u][:, :], xt_hi[u][:, :].bitcast(F32),
                                      ALU.subtract).then_inc(xt_lo_ready, 1)
                    dve.tensor_copy(slot_gate[:, ds(n, 1)], xg[u][:, ds(e + D, 1)]).then_inc(gate_ready, 1)
                if works(n, 1):
                    e = expert_at(dve, n - 1)
                    dve.wait_ge(h_done, n)
                    if not isinstance(n, int) or n >= 3:
                        dve.wait_ge(h_ready, n - 2)
                    dve.tensor_tensor(h_sum[v][:, :], h_bank[:, 0:FE], b1_all[:, ds(e * FE, FE)],
                                      ALU.add).then_inc(h_sum_ready, 1)
                if works(n, 2):
                    dve.wait_ge(ht_hi_ready, n - 1)
                    dve.tensor_tensor(ht_lo[u][:, :], ht_bank[:, 0:FE], ht_hi[u][:, :].bitcast(F32),
                                      ALU.subtract).then_inc(ht_lo_ready, 1)

            slots(0, 0, 1)
            take_logits(TILES - 1)
            first_half(1)
            dve.wait_ge(bias_in[0], 16)
            slots(1, 1, 1)
            second_half(1)
            place_group(1)
            slots(2, 0, 2)
            slots(3, 1, 2)
            dve.wait_ge(bias_in[1], 32)
            slots(4, 0, 3)
            map_group(1)
            index_group(1)
            dve.wait_ge(index_ready, 4)
            over(dve, SLOT_TILES + 4, PEELED, (SLOT_TILES - PEELED) // 2 * 2, slots, start=5)


_TENSORS = ["x_rows", "adj_rows", "adjt_rows", "adjt_cols", "weights", "router_w", "router_b", "b1", "b2"]


def kernel(x, adj, L0_ffn_router_w, L0_ffn_router_b, L0_ffn_W1, L0_ffn_b1, L0_ffn_W2, L0_ffn_b2):
    import numpy as np
    import concourse.bacc as bacc
    from concourse.bass_utils import run_bass_kernel_spmd

    adj_pad = np.pad(np.asarray(adj), ((0, NP - N), (0, NP - N)))
    adjt = np.ascontiguousarray(adj_pad.T)
    w1 = np.asarray(L0_ffn_W1).reshape(E, DC, P, FE).transpose(2, 0, 1, 3).reshape(P, W2_CHUNK, CHUNK)
    w2 = np.asarray(L0_ffn_W2).reshape(E, FC, P, D).transpose(2, 0, 1, 3).reshape(P, CHUNKS - W2_CHUNK, CHUNK)
    arrays = {
        "x_rows": np.pad(np.asarray(x), ((0, NP - N), (0, 0))),
        "adj_rows": adj_pad,
        "adjt_rows": adjt,
        "adjt_cols": adjt.reshape(TILES, P, TILES, P).transpose(2, 1, 0, 3).reshape(NP, NP),
        "weights": np.concatenate([w1, w2], 1).transpose(1, 0, 2).reshape(CHUNKS * P, CHUNK),
        "router_w": np.asarray(L0_ffn_router_w).reshape(DC, P, E).transpose(1, 0, 2),
        "router_b": np.asarray(L0_ffn_router_b).reshape(1, E),
        "b1": np.asarray(L0_ffn_b1).reshape(1, E * FE),
        "b2": np.asarray(L0_ffn_b2).reshape(1, E * D),
    }
    arrays = {n: np.ascontiguousarray(a) for n, a in arrays.items()}
    nc = bacc.Bacc("TRN2", target_bir_lowering=False, num_devices=1)
    args = [nc.dram_tensor(f"{n}_dram", arrays[n].shape, F32, kind="ExternalInput").ap() for n in _TENSORS]
    out = nc.dram_tensor("out_dram", [OUT_ROWS, D], F32, kind="ExternalOutput").ap()
    build(nc, *args, out)
    result = run_bass_kernel_spmd(nc, [{f"{n}_dram": a for n, a in arrays.items()}], core_ids=[0])
    return result.results[0]["out_dram"][:N]
```
